# Optimizing a Trainium2 kernel written in Bass

```python
import numpy as np
import jax
import jax.numpy as jnp

def _softmax(x, axis=-1):
    return jax.nn.softmax(x, axis=axis)

def _gelu(x):
    return jax.nn.gelu(x, approximate=True)

def _silu(x):
    return jax.nn.silu(x)

def _sigmoid(x):
    return jax.nn.sigmoid(x)

def _layernorm(x, axis=-1, eps=1e-05):
    m = jnp.mean(x, axis=axis, keepdims=True)
    v = jnp.var(x, axis=axis, keepdims=True)
    return (x - m) / jnp.sqrt(v + eps)

def _scatter_add(tgt, idx, src, axis=0):
    return tgt.at[idx].add(src)

def _segment_sum(src, seg, n):
    return jax.ops.segment_sum(src, seg, n)
kernel_name = 'mk_gnn_ffn_d1_gnn_r8_70937a'

def setup_inputs(seed: int=0):
    np.random.seed(seed)
    _w = jnp.asarray

    def _rec_inputs():
        import jax
        import jax.numpy as jnp
        _gk = jax.random.key(seed)
        x = -0.0006008 + 1.001 * jax.random.normal(jax.random.fold_in(_gk, 1), (6250, 256), jnp.float32)
        _s = jax.random.randint(jax.random.fold_in(_gk, 2), (50000,), 0, 6250, jnp.int32)
        _d = jax.random.randint(jax.random.fold_in(_gk, 3), (50000,), 0, 6250, jnp.int32)
        _loop = jnp.arange(6250, dtype=jnp.int32)
        src = jnp.concatenate([_s, _d, _loop])
        dst = jnp.concatenate([_d, _s, _loop])
        _o = jnp.argsort(dst, stable=True)
        src = src[_o]
        dst = dst[_o]
        edge_attr_64 = 0.000279952 + 1.00013 * jax.random.normal(jax.random.fold_in(_gk, 11), (106250, 64), jnp.float32)
        return (x, src, dst, edge_attr_64)
    x, src, dst, edge_attr_64 = _rec_inputs()

    def _L0_gnn_setup():
        import jax, jax.numpy as jnp
        import numpy as np
        N_NODES = 1250
        N_EDGES = 40000
        DIM = 256
        EDGE_DIM = 64
        HEADS = 4
        HEAD_DIM = DIM // HEADS
        K_HOPS = 3
        GAMMA = 0.5
        FF_HIDDEN = 512
        key = jax.random.key(seed)
        ks = jax.random.split(key, 8)
        x = jax.random.normal(ks[0], (N_NODES, DIM), dtype=jnp.float32)
        edge_index = jax.random.randint(ks[1], (2, N_EDGES), 0, N_NODES, dtype=jnp.int64)
        edge_attr = jax.random.normal(ks[2], (N_EDGES, EDGE_DIM), dtype=jnp.float32)
        W_x = jax.random.normal(ks[3], (DIM, DIM), dtype=jnp.float32) / np.sqrt(DIM)
        W_e = jax.random.normal(ks[4], (EDGE_DIM, DIM), dtype=jnp.float32) / np.sqrt(EDGE_DIM)
        att_a = jax.random.normal(ks[5], (HEADS, HEAD_DIM), dtype=jnp.float32) / np.sqrt(HEAD_DIM)
        W_ff1 = jax.random.normal(ks[6], (DIM, FF_HIDDEN), dtype=jnp.float32) / np.sqrt(DIM)
        W_ff2 = jax.random.normal(ks[7], (FF_HIDDEN, DIM), dtype=jnp.float32) / np.sqrt(FF_HIDDEN)
        return {'x': x, 'edge_index': edge_index, 'edge_attr': edge_attr, 'W_x': W_x, 'W_e': W_e, 'att_a': att_a, 'W_ff1': W_ff1, 'W_ff2': W_ff2}
    _L0_gnn_all = _L0_gnn_setup()
    _L0_gnn_in = {k: v for k, v in _L0_gnn_all.items() if k in ('W_x', 'W_e', 'att_a', 'W_ff1', 'W_ff2')}
    del _L0_gnn_all

    def _L0_ffn_setup():
        import jax, jax.numpy as jnp
        import numpy as np
        B, S, D = (8, 512, 256)
        H = 4 * D
        CAPACITY = 0.5
        key = jax.random.key(seed)
        ks = jax.random.split(key, 6)
        x = jax.random.normal(ks[0], (B, S, D), dtype=jnp.float32)
        attention_mask = jnp.zeros((B, 1, 1, S), dtype=jnp.float32)
        wr = jax.random.normal(ks[1], (D, 1), dtype=jnp.float32) * 0.02
        br = jnp.zeros((1,), dtype=jnp.float32)
        w1 = jax.random.normal(ks[2], (D, H), dtype=jnp.float32) * 0.02
        b1 = jnp.zeros((H,), dtype=jnp.float32)
        w2 = jax.random.normal(ks[3], (H, D), dtype=jnp.float32) * 0.02
        b2 = jnp.zeros((D,), dtype=jnp.float32)
        return {'x': x, 'attention_mask': attention_mask, 'wr': wr, 'br': br, 'w1': w1, 'b1': b1, 'w2': w2, 'b2': b2}
    _L0_ffn_all = _L0_ffn_setup()
    _L0_ffn_in = {k: v for k, v in _L0_ffn_all.items() if k in ('attention_mask', 'wr', 'br', 'w1', 'b1', 'w2', 'b2')}
    del _L0_ffn_all
    return {'x': x, 'src': src, 'dst': dst, 'edge_attr_64': edge_attr_64, 'L0_gnn_W_x': _L0_gnn_in['W_x'], 'L0_gnn_W_e': _L0_gnn_in['W_e'], 'L0_gnn_att_a': _L0_gnn_in['att_a'], 'L0_gnn_W_ff1': _L0_gnn_in['W_ff1'], 'L0_gnn_W_ff2': _L0_gnn_in['W_ff2'], 'L0_ffn_attention_mask': _L0_ffn_in['attention_mask'], 'L0_ffn_wr': _L0_ffn_in['wr'], 'L0_ffn_br': _L0_ffn_in['br'], 'L0_ffn_w1': _L0_ffn_in['w1'], 'L0_ffn_b1': _L0_ffn_in['b1'], 'L0_ffn_w2': _L0_ffn_in['w2'], 'L0_ffn_b2': _L0_ffn_in['b2']}

def reference(x, src, dst, edge_attr_64, L0_gnn_W_x, L0_gnn_W_e, L0_gnn_att_a, L0_gnn_W_ff1, L0_gnn_W_ff2, L0_ffn_attention_mask, L0_ffn_wr, L0_ffn_br, L0_ffn_w1, L0_ffn_b1, L0_ffn_w2, L0_ffn_b2):
    import jax
    import jax.numpy as jnp

    def _L0_gnn_ref(x, edge_index, edge_attr, W_x, W_e, att_a, W_ff1, W_ff2):
        import jax, jax.numpy as jnp
        import numpy as np
        N_NODES = 1250
        N_EDGES = 40000
        DIM = 256
        EDGE_DIM = 64
        HEADS = 4
        HEAD_DIM = DIM // HEADS
        K_HOPS = 3
        GAMMA = 0.5
        FF_HIDDEN = 512
        N = x.shape[0]
        src, dst = (edge_index[0], edge_index[1])
        h0 = x @ W_x
        e = edge_attr @ W_e
        deg = jax.ops.segment_sum(jnp.ones_like(src, dtype=x.dtype), dst, num_segments=N)
        hops = [h0]
        h_prev2 = jnp.zeros_like(h0)
        h_prev1 = h0
        for _ in range(K_HOPS):
            m = jax.nn.relu(h_prev1[src] + e)
            agg = jax.ops.segment_sum(m, dst, num_segments=N)
            h_k = agg - GAMMA * deg[:, None] * h_prev2
            hops.append(h_k)
            h_prev2, h_prev1 = (h_prev1, h_k)
        hs = jnp.stack(hops, 0).reshape(K_HOPS + 1, N, HEADS, HEAD_DIM)
        q = hs[0]
        scores = jnp.einsum('hd,knhd->knh', att_a, jnp.tanh(hs + q[None]))
        alpha = jax.nn.softmax(scores, axis=0)
        out = jnp.einsum('knh,knhd->nhd', alpha, hs).reshape(N, DIM)
        out = out + jax.nn.relu(out @ W_ff1) @ W_ff2
        out = jax.nn.relu(out)
        return x + out

    def _L0_ffn_ref(x, attention_mask, wr, br, w1, b1, w2, b2):
        import jax, jax.numpy as jnp
        import numpy as np
        B, S, D = (8, 512, 256)
        H = 4 * D
        CAPACITY = 0.5
        b, s, d = x.shape
        weights = (jnp.einsum('bsd,do->bso', x, wr) + br)[..., 0]
        k = max(1, int(CAPACITY * s))
        kk = k - 1 if k > 1 else 1
        _, idx = jax.lax.top_k(weights, k)
        sel_idx = idx[:, :kk]
        sel = jnp.take_along_axis(x, sel_idx[:, :, None], axis=1)
        h = jax.nn.gelu(jnp.einsum('bkd,dh->bkh', sel, w1) + b1)
        y = jnp.einsum('bkh,hd->bkd', h, w2) + b2
        w_sel = jnp.take_along_axis(weights, sel_idx, axis=1)
        y = y * w_sel[..., None]
        batch_idx = jnp.arange(b)[:, None]
        processed = jnp.zeros_like(x).at[batch_idx, sel_idx].set(y)
        return processed + x
    edge_index = jnp.stack([src, dst])
    x = x + _L0_gnn_ref(_layernorm(x, axis=-1), edge_index, edge_attr_64, L0_gnn_W_x, L0_gnn_W_e, L0_gnn_att_a, L0_gnn_W_ff1, L0_gnn_W_ff2)
    x = x + _L0_ffn_ref(_layernorm(x, axis=-1)[None], L0_ffn_attention_mask, L0_ffn_wr, L0_ffn_br, L0_ffn_w1, L0_ffn_b1, L0_ffn_w2, L0_ffn_b2)[0]
    return x

_drawn_inputs = setup_inputs


def setup_inputs(seed=0):
    import zlib

    import numpy as np

    out = dict(_drawn_inputs(seed))
    spreads = {'L0_ffn_b1': (0.0, 2.0), 'L0_ffn_b2': (0.0, 2.0)}
    factors = {'L0_ffn_wr': 42.706, 'L0_ffn_w1': 64.0, 'L0_ffn_w2': 64.0}
    for name, (base, spread) in spreads.items():
        noise = np.random.default_rng([zlib.crc32(name.encode()), seed]).standard_normal(out[name].shape)
        drawn = base * np.exp(spread * noise) if base else spread * noise
        out[name] = jnp.asarray(drawn.astype(out[name].dtype))
    for name, factor in factors.items():
        out[name] = (out[name] * factor).astype(out[name].dtype)
    return out
```

```python
from contextlib import ExitStack

import concourse.bass as bass
from concourse import mybir

P = 128
DIM = 256
CH = DIM // P
EDGE_DIM = 64
HEADS = 4
HEAD_DIM = DIM // HEADS
HOPS = 3
GAMMA = 0.5
FF = 512
FFJ = FF // P
HID = 1024
HJ = HID // P
EPS = 1e-5
N = 6250
WINDOWS = -(-N // P)
NP = WINDOWS * P
TAIL = N - (WINDOWS - 1) * P
E = 106250
TILES_IN_GROUP = 4
GROUP = TILES_IN_GROUP * P
RING = 4
POOL_UNROLL = 2 * RING
GROUPS = -(-E // (GROUP * POOL_UNROLL)) * POOL_UNROLL
TILES = GROUPS * TILES_IN_GROUP
EP = TILES * P
VISITS = GROUPS + WINDOWS - 1
SELECTED = N // 2 - 1
WCOL = DIM + 1
BLOCK = 4
BLOCKS = WINDOWS // BLOCK
LOWEST = -3.0e38

ALU = mybir.AluOpType
ACT = mybir.ActivationFunctionType
AX = mybir.AxisListType.X
F32 = mybir.dt.float32
I32 = mybir.dt.int32


def build(nc, x, src, dst, group_last, edges, W_x, W_e, att, W_ff1, W_ff2, wr, br, w1, b1, w2, b2, out):
    with ExitStack() as ctx:
        def sb(name, shape, dt=F32):
            return ctx.enter_context(nc.sbuf_tensor(name, shape, dt))

        def sem(name):
            return ctx.enter_context(nc.semaphore(name))

        tables = [nc.dram_tensor(f"hop_table{k}", (NP, DIM), F32, kind="Internal").ap() for k in range(HOPS)]
        x_plus_ln = nc.dram_tensor("x_plus_ln", (NP, DIM), F32, kind="Internal").ap()

        even = sb("even", [P, WINDOWS, DIM])
        odd = sb("odd", [P, WINDOWS, WCOL])
        neighbours = sb("neighbours", [P, RING, TILES_IN_GROUP, DIM])
        edge_ring = sb("edge_ring", [P, RING, 2, P])
        sums = sb("sums", [P, 2, TILES_IN_GROUP, DIM])
        messages = sb("messages", [P, 2, TILES_IN_GROUP, WCOL])
        onehot = sb("onehot", [P, 2, TILES_IN_GROUP, P])
        src_all = sb("src_all", [P, TILES], I32)
        src_now = sb("src_now", [P, 2, RING * TILES_IN_GROUP], I32)
        dst_int = sb("dst_int", [P, TILES], I32)
        dst_all = sb("dst_all", [P, TILES])
        last_dst = sb("last_dst", [1, GROUPS], I32)
        first_window = sb("first_window", [1, GROUPS + 1], I32)
        node_row = sb("node_row", [P, P])
        window_base = sb("window_base", [P, WINDOWS])
        ident = sb("ident", [P, P])
        zeros = sb("zeros", [P, DIM])
        ones = sb("ones", [P, P])
        below = sb("below", [P, P])
        wx_sb = sb("wx_sb", [P, CH, DIM])
        we_sb = sb("we_sb", [P, DIM])
        wff1_sb = sb("wff1_sb", [P, CH, FF])
        wff2_sb = sb("wff2_sb", [P, FFJ, DIM])
        w1_sb = sb("w1_sb", [P, CH, HID])
        w2_sb = sb("w2_sb", [P, HJ, DIM])
        b1_sb = sb("b1_sb", [P, HJ])
        rows = sb("rows", [1, 3 * DIM + 1])
        rows_all = sb("rows_all", [P, 3 * DIM + 1])
        att_all = rows_all[:, 0:DIM]
        wr_all = rows_all[:, DIM:2 * DIM]
        b2_all = rows_all[:, 2 * DIM:3 * DIM]
        br_all = rows_all[:, 3 * DIM:3 * DIM + 1]
        half_degree = sb("half_degree", [P, WINDOWS])
        stats = sb("stats", [P, 16])
        moment = sb("moment", [P, 2 * WINDOWS])
        roots = sb("roots", [P, WINDOWS])
        root_t = sb("root_t", [P, WINDOWS])
        root_v = sb("root_v", [P, WINDOWS])
        ring_flat = neighbours[:].rearrange("p r t d -> p (r t d)")
        sums_flat = sums[:].rearrange("p r t d -> p (r t d)")
        normal = ring_flat[:, 0:DIM]
        normal_T = ring_flat[:, DIM:2 * DIM]
        residual = ring_flat[:, 2 * DIM:3 * DIM]

        e_ps = ctx.enter_context(nc.psum_tensor("e_ps", [P, 2, TILES_IN_GROUP * DIM], F32))
        sum_ps = ctx.enter_context(nc.psum_tensor("sum_ps", [P, 2, 512], F32))
        more_ps = ctx.enter_context(nc.psum_tensor("more_ps", [P, 2, 512], F32))

        x_landed = sem("x_landed")
        tables_landed = sem("tables_landed")
        weights_landed = sem("weights_landed")
        rows_landed = sem("rows_landed")
        consts_made = sem("consts_made")
        CONSTS = 11
        rows_made = sem("rows_made")
        dve_step = sem("dve_step")
        normal_made = sem("normal_made")
        normal_turned = sem("normal_turned")
        normal_T_made = sem("normal_T_made")
        h0_summed = sem("h0_summed")
        h0_made = sem("h0_made")
        residual_made = sem("residual_made")
        residual_stored = sem("residual_stored")
        published = sem("published")
        edge_landed = [sem(f"edge_landed{r}") for r in range(RING)]
        gathered = [sem(f"gathered{r}") for r in range(RING)]
        src_staged = sem("src_staged")
        edge_multiplied = sem("edge_multiplied")
        added = sem("added")
        relued = sem("relued")
        onehot_ready = sem("onehot_ready")
        scattered = sem("scattered")
        flushed = sem("flushed")
        window_done = sem("window_done")
        hop_started = sem("hop_started")

        block = ctx.enter_context(nc.Block())

        def rolled(eng, n, body, head):
            for i in range(head):
                body(i)
            with eng.Fori(head, n) as i:
                body(i)

        def after(eng, s, count):
            if not (isinstance(count, int) and count <= 0):
                eng.wait_ge(s, count)

        def window(ap, w, width, n):
            return ap[:, bass.ds(w * width, n)]

        even_flat = even[:].rearrange("p w d -> p (w d)")
        odd_flat = odd[:].rearrange("p w d -> p (w d)")

        def state(k, w, n=DIM):
            return window(even_flat, w, DIM, n) if k % 2 == 0 else window(odd_flat, w, WCOL, n)

        def dram_rows(t, w):
            return t[bass.ds(w * P, P), :]

        early = ring_flat[:, 0:2 * DIM]
        xln = ring_flat[:, 2 * DIM:3 * DIM]
        query = ring_flat[:, 3 * DIM:6 * DIM]
        weighed = ring_flat[:, 8 * DIM:12 * DIM]
        attended = ring_flat[:, 12 * DIM:13 * DIM]
        attended_T = ring_flat[:, 13 * DIM:14 * DIM]
        tanhs = sums_flat[:, 0:4 * DIM]
        scaled = sums_flat[:, 4 * DIM:8 * DIM]
        messages_flat = messages[:].rearrange("p r t d -> p (r t d)")
        hidden_T = messages_flat[:, 0:FF]
        ffsum = messages_flat[:, FF:FF + DIM]
        x1 = messages_flat[:, FF + DIM:FF + 2 * DIM]
        x1_ln = messages_flat[:, FF + 2 * DIM:FF + 3 * DIM]
        product = messages_flat[:, FF + 3 * DIM:FF + 4 * DIM]
        score = sb("score", [P, 4 * HEADS])
        maxs = sb("maxs", [P, HEADS])
        less = sb("less", [P, 4 * HEADS])
        exps = sb("exps", [P, 4 * HEADS])
        denominator = sb("denominator", [P, 2 * HEADS])
        alpha = sb("alpha", [P, 4 * HEADS])
        mlp_weight = sb("mlp_weight", [P, WINDOWS])
        attended_T_ps = e_ps[:, 0, 0:DIM]
        hidden_ps = e_ps[:, 0, 512:1024]
        ffsum_ps = e_ps[:, 1, 0:DIM]
        x1_T_ps = e_ps[:, 1, 512:512 + DIM]

        early_landed = sem("early_landed")
        xln_landed = sem("xln_landed")
        queries_made = sem("queries_made")
        tanhs_made = sem("tanhs_made")
        less_made = sem("less_made")
        exps_made = sem("exps_made")
        alpha_made = sem("alpha_made")
        scaled_made = sem("scaled_made")
        attended_made = sem("attended_made")
        attended_turned = sem("attended_turned")
        attended_T_made = sem("attended_T_made")
        hidden_summed = sem("hidden_summed")
        hidden_made = sem("hidden_made")
        ff_summed = sem("ff_summed")
        x1_made = sem("x1_made")
        x1_ln_made = sem("x1_ln_made")
        x1_turned = sem("x1_turned")
        x1_T_made = sem("x1_T_made")
        search = sb("search", [P, 16])
        found = sb("found", [P, WINDOWS])
        equals = sb("equals", [P, WINDOWS])
        prefix = sb("prefix", [P, WINDOWS])
        chosen = sb("chosen", [P, WINDOWS])
        counts_made = sem("counts_made")
        totals_made = sem("totals_made")
        chosen_made = sem("chosen_made")
        hidden2_T = ring_flat[:, 0:HJ * BLOCK * P].rearrange("p (j n) -> p j n", j=HJ)
        biased = sums_flat[:, 0:2 * DIM]
        result = sums_flat[:, 4 * DIM:8 * DIM].rearrange("p (v d) -> p v d", v=BLOCK)
        mlp1_summed = sem("mlp1_summed")
        gelu_made = sem("gelu_made")
        biased_made = sem("biased_made")
        window_table_made = sem("window_table_made")
        mlp2_summed = sem("mlp2_summed")
        result_made = sem("result_made")
        out_stored = sem("out_stored")
        mlp1_ps = more_ps
        mlp2_ps = sum_ps

        @block.sync
        def _(sp):
            sp.dma_start(odd[:, 0:WINDOWS - 1, 0:DIM],
                         x[0:(WINDOWS - 1) * P, :].rearrange("(w p) d -> p w d", p=P)).then_inc(x_landed, 16)
            sp.wait_ge(consts_made, 1)
            sp.dma_start(odd[0:TAIL, WINDOWS - 1, 0:DIM], x[(WINDOWS - 1) * P:N, :]).then_inc(x_landed, 16)
            sp.dma_start(wx_sb[:], W_x.rearrange("(c p) n -> p c n", p=P)).then_inc(weights_landed, 16)
            for h in range(2):
                sp.dma_start(we_sb[h * EDGE_DIM:(h + 1) * EDGE_DIM, :], W_e).then_inc(weights_landed, 16)
            sp.dma_start(src_all[:], src).then_inc(tables_landed, 16)
            sp.dma_start(dst_int[:], dst).then_inc(tables_landed, 16)
            sp.dma_start(last_dst[:], group_last).then_inc(tables_landed, 16)
            sp.dma_start(wff1_sb[:], W_ff1.rearrange("(c p) n -> p c n", p=P)).then_inc(weights_landed, 16)
            sp.dma_start(wff2_sb[:], W_ff2.rearrange("(c p) n -> p c n", p=P)).then_inc(weights_landed, 16)
            sp.dma_start(w1_sb[:], w1.rearrange("(c p) n -> p c n", p=P)).then_inc(weights_landed, 16)
            sp.dma_start(w2_sb[:], w2.rearrange("(c p) n -> p c n", p=P)).then_inc(weights_landed, 16)
            with nc.allow_non_contiguous_dma(reason="1024 numbers, once"):
                sp.dma_start(b1_sb[:], b1.rearrange("(j p) -> p j", p=P)).then_inc(weights_landed, 16)
            sp.dma_start(rows[:, 0:DIM], att).then_inc(rows_landed, 16)
            sp.dma_start(rows[:, DIM:2 * DIM], wr).then_inc(rows_landed, 16)
            sp.dma_start(rows[:, 2 * DIM:3 * DIM], b2).then_inc(rows_landed, 16)
            sp.dma_start(rows[:, 3 * DIM:3 * DIM + 1], br).then_inc(rows_landed, 16)

            with sp.Fori(0, WINDOWS) as w:
                sp.wait_ge(residual_made, w + 1)
                sp.dma_start(dram_rows(x_plus_ln, w), residual).then_inc(residual_stored, 16)
                sp.wait_ge(h0_made, w + 1)
                sp.dma_start(dram_rows(tables[0], w), state(0, w)).then_inc(published, 16)

            for k in range(HOPS - 1):
                with sp.Fori(0, WINDOWS) as w:
                    sp.wait_ge(window_done, w + (k * WINDOWS + 1))
                    sp.dma_start(dram_rows(tables[k + 1], w), state(k + 1, w)).then_inc(published, 16)

            sp.wait_ge(published, 16 * WINDOWS * HOPS)
            sp.wait_ge(residual_stored, 16 * WINDOWS)
            sp.wait_ge(added, RING + HOPS * GROUPS)

            def load(w):
                after(sp, queries_made, w)
                after(sp, scaled_made, w)
                sp.dma_start(early[:, 0:DIM], dram_rows(tables[0], w)).then_inc(early_landed, 16)
                sp.dma_start(early[:, DIM:2 * DIM], dram_rows(tables[1], w)).then_inc(early_landed, 16)
                after(sp, x1_made, w)
                sp.dma_start(xln, dram_rows(x_plus_ln, w)).then_inc(xln_landed, 16)

            rolled(sp, WINDOWS, load, 1)

            with sp.Fori(0, BLOCKS) as b:
                sp.wait_ge(result_made, b * BLOCK + BLOCK)
                sp.dma_start(out[bass.ds(b * (BLOCK * P), BLOCK * P), :].rearrange("(v p) d -> p v d", p=P),
                             result).then_inc(out_stored, 16)
            sp.wait_ge(result_made, WINDOWS)
            sp.dma_start(out[(WINDOWS - 1) * P:N, :], result[0:TAIL, 0, :]).then_inc(out_stored, 16)
            sp.wait_ge(out_stored, 16 * (BLOCKS + 1))

        @block.gpsimd
        def _(pool):
            nc.gpsimd.memset(odd[:, WINDOWS - 1, :], 0.0).then_inc(consts_made, 1)
            nc.gpsimd.memset(ident[:], 0.0).then_inc(consts_made, 1)
            nc.gpsimd.memset(below[:], 1.0).then_inc(consts_made, 1)
            pool.wait_ge(consts_made, 3)
            nc.gpsimd.affine_select(out=ident[:], in_=ident[:], compare_op=ALU.not_equal, fill=1.0, base=0,
                                    pattern=[[-1, P]], channel_multiplier=1).then_inc(consts_made, 1)
            nc.gpsimd.affine_select(out=below[:], in_=below[:], compare_op=ALU.is_gt, fill=0.0, base=0,
                                    pattern=[[1, P]], channel_multiplier=-1).then_inc(consts_made, 1)
            nc.gpsimd.iota(node_row[:], pattern=[[1, P]], base=0, channel_multiplier=0,
                           allow_small_or_imprecise_dtypes=True).then_inc(consts_made, 1)
            nc.gpsimd.iota(window_base[:], pattern=[[P, WINDOWS]], base=0, channel_multiplier=0,
                           allow_small_or_imprecise_dtypes=True).then_inc(consts_made, 1)
            nc.gpsimd.memset(messages[:], 1.0).then_inc(consts_made, 1)
            nc.gpsimd.memset(first_window[:, 0:1], 0).then_inc(consts_made, 1)
            nc.gpsimd.memset(ones[:], 1.0).then_inc(consts_made, 1)
            nc.gpsimd.memset(zeros[:], 0.0).then_inc(consts_made, 1)
            pool.wait_ge(rows_landed, 64)
            nc.gpsimd.partition_broadcast(rows_all[:], rows[:], channels=P).then_inc(rows_made, 1)
            pool.wait_ge(tables_landed, 48)
            for k in range(HOPS):
                pool.wait_ge(published, 16 * WINDOWS * (k + 1))
                if k == 0:
                    pool.wait_ge(residual_stored, 16 * WINDOWS)
                    pool.wait_ge(h0_summed, WINDOWS)
                with pool.Fori(0, GROUPS // POOL_UNROLL) as it:
                    for u in range(POOL_UNROLL):
                        r = u % RING
                        g = it * POOL_UNROLL + u + k * GROUPS
                        half = u // RING
                        pool.wait_ge(added, g + 1)
                        if r == 0:
                            pool.nop(nofuse=True)
                            cols = bass.ds(it * (POOL_UNROLL * TILES_IN_GROUP) + half * RING * TILES_IN_GROUP,
                                           RING * TILES_IN_GROUP)
                            nc.gpsimd.tensor_copy(src_now[:, half, :], src_all[:, cols]).then_inc(src_staged, 1)
                            pool.wait_ge(src_staged, it * 2 + (half + 1 + 2 * k * (GROUPS // POOL_UNROLL)))
                        pool.nop(nofuse=True)
                        for t in range(TILES_IN_GROUP):
                            i = r * TILES_IN_GROUP + t
                            nc.gpsimd.indirect_dma_start(
                                out=neighbours[:, r, t, :], out_offset=None, in_=tables[k],
                                in_offset=bass.IndirectOffsetOnAxis(ap=src_now[:, half, i:i + 1], axis=0),
                            ).then_inc(gathered[r], 16)

        @block.scalar
        def _(act):
            def turn_copy(w):
                act.wait_ge(normal_turned, w + 1)
                after(act, h0_summed, w)
                nc.scalar.copy(normal_T, e_ps[:, 0, 0:DIM]).then_inc(normal_T_made, 1)

            rolled(act, WINDOWS, turn_copy, 1)

            def load_edges(k, g, u):
                act.wait_ge(edge_multiplied, g + (k * GROUPS + 1))
                act.dma_start(edge_ring[:, u % RING],
                              edges[:, bass.ds(g * 2 * P, 2 * P)].rearrange("p (j e) -> p j e", j=2)
                              ).then_inc(edge_landed[u % RING], 16)

            act.sem_inc(relued, 2)
            for k in range(HOPS):
                load_edges(k, 0, 0)
                load_edges(k, 1, 1)

                def rectify(it, last):
                    for u in range(RING):
                        g = it * RING + u
                        if not last or u + 2 < RING:
                            load_edges(k, g + 2, u + 2)
                        act.wait_ge(added, g + (RING + k * GROUPS + 1))
                        if k == 0 and u < 2:
                            act.wait_ge(consts_made, CONSTS)
                        nc.scalar.activation(messages[:, u % 2, :, 0:DIM], sums[:, u % 2], ACT.Relu).then_inc(relued, 1)

                with act.Fori(0, GROUPS // RING - 1) as it:
                    rectify(it, False)
                rectify(GROUPS // RING - 1, True)

            def attend(w):
                act.wait_ge(early_landed, w * 32 + 32)
                act.wait_ge(queries_made, w + 1)
                nc.scalar.activation(tanhs[:, 0:DIM], early[:, 0:DIM], ACT.Tanh, scale=2.0)
                nc.scalar.activation(tanhs[:, DIM:4 * DIM], query, ACT.Tanh).then_inc(tanhs_made, 1)
                act.wait_ge(less_made, w + 1)
                nc.scalar.activation(exps[:], less[:], ACT.Exp).then_inc(exps_made, 1)
                act.wait_ge(alpha_made, w + 1)
                after(act, attended_made, w)
                act.nop(nofuse=True)
                for k in range(HOPS + 1):
                    for h in range(HEADS):
                        source = (early[:, k * DIM + h * HEAD_DIM:k * DIM + (h + 1) * HEAD_DIM] if k < 2
                                  else state(k, w)[:, h * HEAD_DIM:(h + 1) * HEAD_DIM])
                        last = nc.scalar.activation(
                            scaled[:, k * DIM + h * HEAD_DIM:k * DIM + (h + 1) * HEAD_DIM], source, ACT.Copy,
                            scale=alpha[:, k * HEADS + h:k * HEADS + h + 1])
                last.then_inc(scaled_made, 1)
                act.wait_ge(attended_turned, w + 1)
                nc.scalar.copy(attended_T, attended_T_ps).then_inc(attended_T_made, 1)
                act.wait_ge(hidden_summed, w + 1)
                nc.scalar.activation(hidden_T, hidden_ps, ACT.Relu).then_inc(hidden_made, 1)

            def turn_x1(w):
                act.wait_ge(x1_turned, w + 1)
                act.nop(nofuse=True)
                nc.scalar.copy(state(0, w), x1_T_ps).then_inc(x1_T_made, 1)

            def attend_step(w):
                attend(w)
                if not isinstance(w, int) or w:
                    turn_x1(w - 1)

            rolled(act, WINDOWS, attend_step, 1)
            turn_x1(WINDOWS - 1)

            def gelus(b, width):
                for j in range(HJ):
                    act.wait_ge(mlp1_summed, b * HJ + j + 1)
                    if j == 0:
                        after(act, mlp2_summed, b * BLOCK)
                    nc.scalar.activation(hidden2_T[:, j, 0:width], mlp1_ps[:, j % 2, 0:width], ACT.Gelu_apprx_tanh,
                                         bias=b1_sb[:, j:j + 1]).then_inc(gelu_made, 1)

            rolled(act, BLOCKS, lambda b: gelus(b, BLOCK * P), 1)
            gelus(BLOCKS, P)

        @block.vector
        def _(dve):
            steps = [0]

            def step(ins):
                ins.then_inc(dve_step, 1)
                steps[0] += 1
                dve.wait_ge(dve_step, steps[0])

            dve.sem_inc(added, RING)
            dve.sem_inc(flushed, 1)
            dve.wait_ge(consts_made, CONSTS)
            dve.wait_ge(tables_landed, 48)
            nc.vector.tensor_copy(dst_all[:], dst_int[:]).then_inc(dve_step, 1)
            nc.vector.tensor_single_scalar(first_window[:, 1:GROUPS + 1], last_dst[:], P.bit_length() - 1,
                                           op=ALU.arith_shift_right).then_inc(window_table_made, 1)
            steps[0] += 1
            dve.wait_ge(window_table_made, 1)
            dve.wait_ge(x_landed, 32)

            RSQRT = 15

            def rsqrt(link, root, value, t, v):
                link(nc.vector.tensor_scalar(v, value, EPS, None, ALU.add))
                link(nc.vector.tensor_single_scalar(t.bitcast(I32), v.bitcast(I32), 1, op=ALU.logical_shift_right))
                link(nc.vector.tensor_scalar(root.bitcast(I32), t.bitcast(I32), -1.0, float(0x5F3759DF),
                                             ALU.mult, ALU.add))
                link(nc.vector.tensor_tensor(t, root, root, ALU.mult))
                for i in range(3):
                    link(nc.vector.tensor_tensor(t, t, v, ALU.mult))
                    link(nc.vector.tensor_scalar(t, t, -0.5, 1.5, ALU.mult, ALU.add))
                    link(nc.vector.tensor_tensor(root, root, t, ALU.mult))
                    if i < 2:
                        link(nc.vector.tensor_tensor(t, root, root, ALU.mult))

            base_s = steps[0]

            def moments(w):
                nc.vector.bn_stats(stats[:, 0:6], state(1, w)).then_inc(dve_step, 1)
                dve.wait_ge(dve_step, w * 3 + (base_s + 1))
                dve.nop(nofuse=True)
                nc.vector.bn_aggr(stats[:, 6:8], stats[:, 0:6]).then_inc(dve_step, 1)
                dve.wait_ge(dve_step, w * 3 + (base_s + 2))
                nc.vector.tensor_scalar(moment[:, bass.ds(w * 2, 2)], stats[:, 6:8], 1.0, None,
                                        ALU.mult).then_inc(dve_step, 1)
                dve.wait_ge(dve_step, w * 3 + (base_s + 3))

            rolled(dve, WINDOWS, moments, 1)
            steps[0] += 3 * WINDOWS
            rsqrt(step, roots[:], moment[:].rearrange("p (w two) -> p w two", two=2)[:, :, 1], root_t[:], root_v[:])

            LN = 1

            def normalise(w):
                xw = state(1, w)
                after(dve, normal_turned, w)
                nc.vector.tensor_scalar(normal, xw, moment[:, bass.ds(w * 2, 1)], roots[:, bass.ds(w, 1)],
                                        ALU.subtract, ALU.mult).then_inc(normal_made, 1)
                dve.wait_ge(normal_made, w + 1)
                after(dve, residual_stored, w * 16)
                nc.vector.tensor_tensor(residual, normal, xw, ALU.add).then_inc(residual_made, 1)
                dve.wait_ge(residual_made, w + 1)
                nc.vector.tensor_scalar(xw, zeros[:], 1.0, None, ALU.mult).then_inc(dve_step, 1)

            def copy_h0(w):
                dve.wait_ge(h0_summed, w + 1)
                nc.vector.tensor_scalar(state(0, w), e_ps[:, 1, 0:DIM], 1.0, None, ALU.mult).then_inc(h0_made, 1)

            def node_step(w):
                normalise(w)
                if not isinstance(w, int) or w:
                    copy_h0(w - 1)

            rolled(dve, WINDOWS, node_step, 1)
            copy_h0(WINDOWS - 1)
            steps[0] += LN * WINDOWS
            dve.wait_ge(dve_step, steps[0])
            step(nc.vector.memset(odd[:, :, DIM:WCOL], 0.0))

            for k in range(HOPS):
                if k == 1:
                    step(nc.vector.tensor_scalar(half_degree[:], odd[:, :, DIM:WCOL].rearrange("p w o -> p (w o)"),
                                                 -GAMMA, None, ALU.mult))
                if k:
                    dve.wait_ge(published, 16 * WINDOWS * k)
                    with dve.Fori(0, WINDOWS) as w:
                        nc.vector.tensor_scalar(state(k + 1, w), state(k + 1, w), half_degree[:, bass.ds(w, 1)], None,
                                                ALU.mult).then_inc(hop_started, 1)
                    dve.wait_ge(hop_started, k * WINDOWS)
                width = WCOL if k == 0 else DIM

                def add(g, u):
                    dve.wait_ge(edge_multiplied, g + (k * GROUPS + RING + 1))
                    dve.wait_ge(relued, g + (k * GROUPS + 1))
                    use = (g - u % RING) // RING if isinstance(g, int) else None
                    r = u % RING
                    if use is None:
                        use = g_iter[0] + (1 if u >= RING else 0)
                    dve.wait_ge(gathered[r], use * (16 * TILES_IN_GROUP) + 16 * TILES_IN_GROUP * (1 + k * (GROUPS // RING)))
                    nc.vector.tensor_tensor(sums[:, u % 2].rearrange("p t d -> p (t d)"), e_ps[:, u % 2, :],
                                            neighbours[:, r].rearrange("p t d -> p (t d)"), ALU.add).then_inc(added, 1)

                def make_onehot(it, u, w):
                    d = dst_all[:, bass.ds(it * (RING * TILES_IN_GROUP) + u * TILES_IN_GROUP, TILES_IN_GROUP)]
                    nc.vector.scalar_tensor_tensor(
                        out=onehot[:, u % 2],
                        in0=node_row[:].unsqueeze(1).broadcast_to([P, TILES_IN_GROUP, P]),
                        scalar=window_base[:, bass.ds(w, 1)],
                        in1=d.unsqueeze(2).broadcast_to([P, TILES_IN_GROUP, P]),
                        op0=ALU.add, op1=ALU.is_equal).then_inc(onehot_ready, 1)

                def flush(it, u, w):
                    visit = it * RING + w + (u + k * VISITS)
                    dve.wait_ge(scattered, visit + 1)
                    dve.wait_ge(flushed, visit + 1)
                    acc = state(k + 1, w, width)
                    nc.vector.tensor_tensor(acc, sum_ps[:, u % 2, 0:width], acc, ALU.add).then_inc(flushed, 1)

                g_iter = [0]

                def walk(it, last):
                    g_iter[0] = it
                    ws = [dve.value_load(first_window[:, bass.ds(it * RING + u, 1)], min_val=0, max_val=WINDOWS - 1)
                          for u in range(RING + 1)]
                    for u in range(RING):
                        make_onehot(it, u, ws[u])
                        if not last or u + 1 < RING:
                            add(it * RING + u + 1, u + 1)
                        flush(it, u, ws[u])
                        with dve.If(ws[u] < ws[u + 1]):
                            with dve.Fori(ws[u] + 1, ws[u + 1] + 1) as w:
                                dve.wait_ge(flushed, it * RING + w + (u + k * VISITS + 1))
                                dve.nop(nofuse=True)
                                nc.vector.engine_nop().then_inc(window_done, 1)
                                make_onehot(it, u, w)
                                flush(it, u, w)

                add(0, 0)
                with dve.Fori(0, GROUPS // RING - 1) as it:
                    walk(it, False)
                walk(GROUPS // RING - 1, True)
                dve.wait_ge(flushed, 1 + (k + 1) * VISITS)
                nc.vector.engine_nop().then_inc(window_done, 1)

            DS = 12 + RSQRT
            base1 = steps[0]

            def attend(w):
                base = w * DS + base1
                at = [0]

                def link(ins):
                    ins.then_inc(dve_step, 1)
                    at[0] += 1
                    dve.wait_ge(dve_step, base + at[0])

                dve.wait_ge(early_landed, w * 32 + 32)
                nc.vector.tensor_tensor(query[:, 0:DIM], early[:, DIM:2 * DIM], early[:, 0:DIM], ALU.add)
                nc.vector.tensor_tensor(query[:, DIM:2 * DIM], state(2, w), early[:, 0:DIM], ALU.add)
                nc.vector.tensor_tensor(query[:, 2 * DIM:3 * DIM], state(3, w), early[:, 0:DIM],
                                        ALU.add).then_inc(queries_made, 1)
                dve.wait_ge(tanhs_made, w + 1)
                link(nc.vector.tensor_tensor(weighed.rearrange("p (k d) -> p k d", d=DIM),
                                             tanhs.rearrange("p (k d) -> p k d", d=DIM),
                                             att_all.unsqueeze(1).broadcast_to([P, 4, DIM]), ALU.mult))
                link(nc.vector.tensor_reduce(score[:], weighed.rearrange("p (s d) -> p s d", d=HEAD_DIM), AX, ALU.add))
                link(nc.vector.tensor_reduce(maxs[:], score[:].rearrange("p (k h) -> p h k", h=HEADS), AX, ALU.max))
                nc.vector.tensor_tensor(less[:].rearrange("p (k h) -> p k h", h=HEADS),
                                        score[:].rearrange("p (k h) -> p k h", h=HEADS),
                                        maxs[:].unsqueeze(1).broadcast_to([P, 4, HEADS]),
                                        ALU.subtract).then_inc(less_made, 1)
                dve.wait_ge(exps_made, w + 1)
                link(nc.vector.tensor_reduce(denominator[:, 0:HEADS], exps[:].rearrange("p (k h) -> p h k", h=HEADS),
                                             AX, ALU.add))
                link(nc.vector.reciprocal(denominator[:, HEADS:2 * HEADS], denominator[:, 0:HEADS]))
                nc.vector.tensor_tensor(alpha[:].rearrange("p (k h) -> p k h", h=HEADS),
                                        exps[:].rearrange("p (k h) -> p k h", h=HEADS),
                                        denominator[:, HEADS:2 * HEADS].unsqueeze(1).broadcast_to([P, 4, HEADS]),
                                        ALU.mult).then_inc(alpha_made, 1)
                dve.wait_ge(scaled_made, w + 1)
                link(nc.vector.tensor_tensor(weighed[:, 0:2 * DIM], scaled[:, 0:2 * DIM], scaled[:, 2 * DIM:4 * DIM],
                                             ALU.add))
                nc.vector.tensor_tensor(attended, weighed[:, 0:DIM], weighed[:, DIM:2 * DIM],
                                        ALU.add).then_inc(attended_made, 1)
                dve.wait_ge(ff_summed, w + 1)
                link(nc.vector.tensor_tensor(ffsum, ffsum_ps, attended, ALU.add))
                dve.wait_ge(xln_landed, w * 16 + 16)
                nc.vector.scalar_tensor_tensor(out=x1, in0=ffsum, scalar=0.0, in1=xln, op0=ALU.max,
                                               op1=ALU.add).then_inc(x1_made, 1)
                dve.wait_ge(x1_made, w + 1)
                link(nc.vector.bn_stats(stats[:, 0:6], x1))
                dve.nop(nofuse=True)
                link(nc.vector.bn_aggr(stats[:, 6:8], stats[:, 0:6]))
                rsqrt(link, stats[:, 8:9], stats[:, 7:8], stats[:, 9:10], stats[:, 10:11])
                after(dve, x1_turned, w)
                nc.vector.tensor_scalar(x1_ln, x1, stats[:, 6:7], stats[:, 8:9],
                                        ALU.subtract, ALU.mult).then_inc(x1_ln_made, 1)
                dve.wait_ge(x1_ln_made, w + 1)
                link(nc.vector.tensor_tensor(product, x1_ln, wr_all, ALU.mult))
                link(nc.vector.tensor_reduce(mlp_weight[:, bass.ds(w, 1)], product, AX, ALU.add))
                link(nc.vector.tensor_tensor(state(3, w), x1, x1_ln, ALU.add))
                assert at[0] == DS

            dve.wait_ge(rows_made, 1)
            rolled(dve, WINDOWS, attend, 1)
            steps[0] += DS * WINDOWS

            step(nc.vector.tensor_scalar(mlp_weight[:], mlp_weight[:], br_all, None, ALU.add))
            step(nc.vector.tensor_copy(found[:], mlp_weight[:]))
            step(nc.vector.tensor_reduce(search[:, 0:1], below[:, 0:TAIL], AX, ALU.add))
            step(nc.vector.tensor_scalar(search[:, 1:2], search[:, 0:1], 0.5, None, ALU.is_gt))
            last_w = found[:, WINDOWS - 1:WINDOWS]
            step(nc.vector.tensor_tensor(search[:, 1:2], search[:, 1:2], ident[:, TAIL - 1:TAIL], ALU.add))
            step(nc.vector.tensor_tensor(last_w, last_w, search[:, 1:2], ALU.mult))
            step(nc.vector.tensor_scalar(search[:, 2:3], search[:, 1:2], 1.0, -LOWEST, ALU.subtract, ALU.mult))
            step(nc.vector.tensor_tensor(last_w, last_w, search[:, 2:3], ALU.add))

            magnitude = search[:, 3:4].bitcast(I32)
            candidate = search[:, 4:5].bitcast(I32)
            bit = search[:, 5:6].bitcast(I32)
            signed = search[:, 6:7]
            count = search[:, 7:8]
            enough = search[:, 8:9]
            sign = search[:, 9:10]
            flip = search[:, 10:11]
            keep = search[:, 11:12]
            total_ps = more_ps[:, 0, 0:1]
            asked = [0]

            def total(against, op, values=found):
                step(nc.vector.tensor_scalar(equals[:], values[:], against, None, op))
                nc.vector.tensor_reduce(count, equals[:], AX, ALU.add).then_inc(counts_made, 1)
                asked[0] += 1
                dve.wait_ge(totals_made, asked[0])

            step(nc.vector.memset(search[:, 12:13], 0.0))
            total(search[:, 12:13], ALU.is_ge)
            step(nc.vector.tensor_scalar(enough, total_ps, float(SELECTED), None, ALU.is_ge))
            step(nc.vector.tensor_scalar(sign, enough, 2.0, -1.0, ALU.mult, ALU.add))
            step(nc.vector.tensor_scalar(flip, enough, -1.0, 1.0, ALU.mult, ALU.add))
            step(nc.vector.memset(magnitude, 0))
            step(nc.vector.memset(bit, 1 << 30))

            SS = 9
            base2, asked2 = steps[0], asked[0]
            with dve.Fori(0, 31) as i:
                base = i * SS + base2
                at = [0]

                def link(ins):
                    ins.then_inc(dve_step, 1)
                    at[0] += 1
                    dve.wait_ge(dve_step, base + at[0])

                link(nc.vector.tensor_tensor(candidate, magnitude, bit, ALU.bitwise_or))
                link(nc.vector.tensor_tensor(signed, search[:, 4:5], sign, ALU.mult))
                link(nc.vector.tensor_scalar(equals[:], found[:], signed, None, ALU.is_ge))
                nc.vector.tensor_reduce(count, equals[:], AX, ALU.add).then_inc(counts_made, 1)
                dve.wait_ge(totals_made, i + (asked2 + 1))
                link(nc.vector.tensor_scalar(enough, total_ps, float(SELECTED), None, ALU.is_ge))
                link(nc.vector.tensor_tensor(keep, enough, flip, ALU.not_equal))
                link(nc.vector.tensor_scalar(search[:, 13:14].bitcast(I32), keep, -1.0, None, ALU.mult))
                link(nc.vector.tensor_tensor(search[:, 14:15].bitcast(I32), bit, search[:, 13:14].bitcast(I32),
                                             ALU.bitwise_and))
                link(nc.vector.tensor_tensor(magnitude, magnitude, search[:, 14:15].bitcast(I32), ALU.bitwise_or))
                link(nc.vector.tensor_single_scalar(bit, bit, 1, op=ALU.logical_shift_right))
                assert at[0] == SS
            steps[0] += SS * 31
            asked[0] += 31
            step(nc.vector.tensor_tensor(signed, search[:, 3:4], sign, ALU.mult))
            step(nc.vector.tensor_scalar(equals[:], found[:], signed, None, ALU.is_ge))
            step(nc.vector.tensor_scalar(prefix[:], found[:], signed, None, ALU.is_gt))
            step(nc.vector.tensor_tensor(chosen[:], equals[:], prefix[:], ALU.subtract))
            step(nc.vector.scalar_tensor_tensor(out=prefix[:], in0=chosen[:], scalar=flip, in1=prefix[:],
                                                op0=ALU.mult, op1=ALU.add))
            step(nc.vector.tensor_copy(chosen[:], prefix[:]))
            step(nc.vector.tensor_copy(search[:, 12:13].bitcast(I32), flip))
            step(nc.vector.tensor_scalar(search[:, 13:14].bitcast(I32), magnitude, 65535, None, ALU.bitwise_and))
            step(nc.vector.tensor_scalar(search[:, 14:15].bitcast(I32), magnitude, 16, None, ALU.logical_shift_right))
            step(nc.vector.tensor_tensor(search[:, 13:14].bitcast(I32), search[:, 13:14].bitcast(I32),
                                         search[:, 12:13].bitcast(I32), ALU.add))
            step(nc.vector.tensor_scalar(search[:, 12:13].bitcast(I32), search[:, 13:14].bitcast(I32), 16, None,
                                         ALU.logical_shift_right))
            step(nc.vector.tensor_tensor(search[:, 14:15].bitcast(I32), search[:, 14:15].bitcast(I32),
                                         search[:, 12:13].bitcast(I32), ALU.add))
            step(nc.vector.tensor_scalar(search[:, 14:15].bitcast(I32), search[:, 14:15].bitcast(I32), 16, None,
                                         ALU.logical_shift_left))
            step(nc.vector.tensor_scalar(search[:, 13:14].bitcast(I32), search[:, 13:14].bitcast(I32), 65535, None,
                                         ALU.bitwise_and))
            step(nc.vector.tensor_tensor(search[:, 15:16].bitcast(I32), search[:, 14:15].bitcast(I32),
                                         search[:, 13:14].bitcast(I32), ALU.bitwise_or))
            step(nc.vector.tensor_tensor(signed, search[:, 15:16], sign, ALU.mult))
            step(nc.vector.tensor_scalar(equals[:], found[:], signed, None, ALU.is_equal))
            nc.vector.tensor_reduce(count, chosen[:], AX, ALU.add).then_inc(counts_made, 1)
            asked[0] += 1
            dve.wait_ge(totals_made, asked[0])
            step(nc.vector.tensor_scalar(keep, total_ps, -1.0, float(SELECTED), ALU.mult, ALU.add))
            nc.vector.engine_nop().then_inc(chosen_made, 1)
            dve.wait_ge(chosen_made, 2)
            step(nc.vector.tensor_copy(prefix[:], more_ps[:, 1, 0:WINDOWS]))
            step(nc.vector.memset(half_degree[:], 1.0))
            step(nc.vector.tensor_tensor_scan(out=half_degree[:], data0=half_degree[:],
                                              data1=prefix[:], initial=0.0, op0=ALU.mult, op1=ALU.add))
            step(nc.vector.tensor_tensor(half_degree[:], half_degree[:], prefix[:], ALU.subtract))
            step(nc.vector.tensor_tensor(prefix[:], half_degree[:], more_ps[:, 1, WINDOWS:2 * WINDOWS], ALU.add))
            step(nc.vector.tensor_scalar(prefix[:], prefix[:], keep, None, ALU.is_lt))
            step(nc.vector.tensor_tensor(prefix[:], prefix[:], equals[:], ALU.mult))
            step(nc.vector.tensor_tensor(chosen[:], chosen[:], prefix[:], ALU.add))
            step(nc.vector.tensor_tensor(chosen[:], chosen[:], mlp_weight[:], ALU.mult))
            nc.vector.engine_nop().then_inc(chosen_made, 1)

            def results(b, v):
                n = b * BLOCK + v
                dve.wait_ge(mlp2_summed, n + 1)
                if v == 0:
                    after(dve, out_stored, b * 16)
                half = biased[:, (v % 2) * DIM:(v % 2 + 1) * DIM]
                nc.vector.tensor_tensor(half, mlp2_ps[:, v % 2, 0:DIM], b2_all, ALU.add).then_inc(biased_made, 1)
                dve.wait_ge(biased_made, n + 1)
                nc.vector.scalar_tensor_tensor(out=result[:, v, :], in0=half, scalar=chosen[:, bass.ds(n, 1)],
                                               in1=state(3, n), op0=ALU.mult, op1=ALU.add).then_inc(result_made, 1)

            def results_of_block(b):
                for v in range(BLOCK):
                    results(b, v)

            rolled(dve, BLOCKS, results_of_block, 1)
            results(BLOCKS, 0)

        @block.tensor
        def _(pe):
            pe.sem_inc(edge_multiplied, RING)
            pe.wait_ge(consts_made, CONSTS)
            pe.wait_ge(weights_landed, 16 * 8)

            def turn(w):
                pe.wait_ge(normal_made, w + 1)
                after(pe, normal_T_made, w)
                for c in range(CH):
                    last = nc.tensor.transpose(e_ps[:, 0, c * P:(c + 1) * P], normal[:, c * P:(c + 1) * P], ident[:])
                last.then_inc(normal_turned, 1)

            def project(w):
                pe.wait_ge(normal_T_made, w + 1)
                after(pe, h0_made, w)
                for c in range(CH):
                    last = nc.tensor.matmul(e_ps[:, 1, 0:DIM], normal_T[:, c * P:(c + 1) * P], wx_sb[:, c, :],
                                            start=(c == 0), stop=(c == CH - 1))
                last.then_inc(h0_summed, 1)

            def project_step(w):
                turn(w)
                project(w)

            rolled(pe, WINDOWS, project_step, 1)
            pe.wait_ge(h0_made, WINDOWS)

            for k in range(HOPS):
                width = WCOL if k == 0 else DIM

                def multiply_edges(it, u):
                    r = u % RING
                    use = it + u // RING
                    pe.wait_ge(edge_landed[r], use * 16 + 16 * (1 + k * (GROUPS // RING)))
                    pe.wait_ge(added, it * RING + (u + k * GROUPS + RING - 1))
                    for h in range(2):
                        part = slice(h * EDGE_DIM, (h + 1) * EDGE_DIM)
                        for j in range(2):
                            q = 2 * h + j
                            last = nc.tensor.matmul(e_ps[:, u % 2, q * DIM:(q + 1) * DIM], edge_ring[part, r, j, :],
                                                    we_sb[part, :], start=True, stop=True)
                    last.then_inc(edge_multiplied, 1)

                def scatter(it, u, w):
                    pe.wait_ge(onehot_ready, it * RING + w + (u + k * VISITS + 1))
                    for t in range(TILES_IN_GROUP):
                        last = nc.tensor.matmul(sum_ps[:, u % 2, 0:width], onehot[:, u % 2, t, :],
                                                messages[:, u % 2, t, 0:width], start=(t == 0),
                                                stop=(t == TILES_IN_GROUP - 1))
                    last.then_inc(scattered, 1)

                def walk(it, last):
                    ws = [pe.value_load(first_window[:, bass.ds(it * RING + u, 1)], min_val=0, max_val=WINDOWS - 1)
                          for u in range(RING + 1)]
                    for u in range(RING):
                        if not last or u + 1 < RING:
                            multiply_edges(it, u + 1)
                        pe.wait_ge(relued, it * RING + (u + k * GROUPS + 3))
                        scatter(it, u, ws[u])
                        with pe.If(ws[u] < ws[u + 1]):
                            with pe.Fori(ws[u] + 1, ws[u + 1] + 1) as w:
                                scatter(it, u, w)

                if k == 0:
                    pe.wait_ge(window_table_made, 1)
                multiply_edges(0, 0)
                with pe.Fori(0, GROUPS // RING - 1) as it:
                    walk(it, False)
                walk(GROUPS // RING - 1, True)

            def feed(w):
                pe.wait_ge(attended_made, w + 1)
                for c in range(CH):
                    last = nc.tensor.transpose(attended_T_ps[:, c * P:(c + 1) * P], attended[:, c * P:(c + 1) * P],
                                               ident[:])
                last.then_inc(attended_turned, 1)
                pe.wait_ge(attended_T_made, w + 1)
                for j in range(FFJ):
                    for c in range(CH):
                        last = nc.tensor.matmul(hidden_ps[:, j * P:(j + 1) * P], wff1_sb[:, c, j * P:(j + 1) * P],
                                                attended_T[:, c * P:(c + 1) * P], start=(c == 0), stop=(c == CH - 1))
                last.then_inc(hidden_summed, 1)
                pe.wait_ge(hidden_made, w + 1)
                for j in range(FFJ):
                    last = nc.tensor.matmul(ffsum_ps, hidden_T[:, j * P:(j + 1) * P], wff2_sb[:, j, :],
                                            start=(j == 0), stop=(j == FFJ - 1))
                last.then_inc(ff_summed, 1)
                pe.wait_ge(x1_ln_made, w + 1)
                after(pe, x1_T_made, w)
                for c in range(CH):
                    last = nc.tensor.transpose(x1_T_ps[:, c * P:(c + 1) * P], x1_ln[:, c * P:(c + 1) * P], ident[:])
                last.then_inc(x1_turned, 1)

            rolled(pe, WINDOWS, feed, 1)

            def sum_counts():
                nc.tensor.matmul(more_ps[:, 0, 0:1], ones[:], search[:, 7:8], start=True,
                                 stop=True).then_inc(totals_made, 1)

            pe.wait_ge(counts_made, 1)
            sum_counts()
            with pe.Fori(0, 31) as i:
                pe.wait_ge(counts_made, i + 2)
                sum_counts()
            pe.wait_ge(counts_made, 33)
            sum_counts()
            pe.wait_ge(chosen_made, 1)
            nc.tensor.matmul(more_ps[:, 1, 0:WINDOWS], ones[:], equals[:], start=True, stop=True)
            nc.tensor.matmul(more_ps[:, 1, WINDOWS:2 * WINDOWS], below[:], equals[:], start=True,
                             stop=True).then_inc(chosen_made, 1)
            pe.wait_ge(chosen_made, 3)
            pe.wait_ge(x1_T_made, WINDOWS)

            x1_T = even[:].rearrange("p w d -> p (w d)")

            def mlp(b, windows):
                n = windows * P
                for j in range(HJ):
                    after(pe, gelu_made, b * HJ + j - 1)
                    for c in range(CH):
                        if windows == 1:
                            rhs = x1_T[:, b * BLOCK * DIM + c * P:b * BLOCK * DIM + (c + 1) * P]
                        else:
                            rhs = x1_T[:, bass.ds(b * (BLOCK * DIM), BLOCK * DIM)].rearrange(
                                "p (v d) -> p v d", v=BLOCK)[:, :, c * P:(c + 1) * P]
                        last = nc.tensor.matmul(mlp1_ps[:, j % 2, 0:n], w1_sb[:, c, j * P:(j + 1) * P], rhs,
                                                start=(c == 0), stop=(c == CH - 1))
                    last.then_inc(mlp1_summed, 1)
                pe.wait_ge(gelu_made, b * HJ + HJ)
                for v in range(windows):
                    after(pe, biased_made, b * BLOCK + v - 1)
                    for j in range(HJ):
                        last = nc.tensor.matmul(mlp2_ps[:, v % 2, 0:DIM], hidden2_T[:, j, v * P:(v + 1) * P],
                                                w2_sb[:, j, :], start=(j == 0), stop=(j == HJ - 1))
                    last.then_inc(mlp2_summed, 1)

            rolled(pe, BLOCKS, lambda b: mlp(b, BLOCK), 1)
            mlp(BLOCKS, 1)


def kernel(x, src, dst, edge_attr_64, L0_gnn_W_x, L0_gnn_W_e, L0_gnn_att_a, L0_gnn_W_ff1, L0_gnn_W_ff2,
           L0_ffn_attention_mask, L0_ffn_wr, L0_ffn_br, L0_ffn_w1, L0_ffn_b1, L0_ffn_w2, L0_ffn_b2):
    import numpy as np
    import concourse.bacc as bacc
    from concourse.bass_utils import run_bass_kernel_spmd

    def padded(a, fill):
        a = np.asarray(a)
        return np.concatenate([a, np.full((EP - E,) + a.shape[1:], fill, a.dtype)])

    src_p, dst_p = padded(src, 0), padded(dst, NP - 1)
    edges = padded(edge_attr_64, 0).reshape(GROUPS, 2, 2, P, EDGE_DIM).transpose(1, 4, 0, 2, 3)
    arrays = {
        "x": x, "src": src_p.reshape(TILES, P).T, "dst": dst_p.reshape(TILES, P).T,
        "group_last": dst_p[GROUP - 1::GROUP].reshape(1, GROUPS),
        "edges": edges.reshape(2 * EDGE_DIM, GROUPS * 2 * P),
        "W_x": L0_gnn_W_x, "W_e": L0_gnn_W_e, "att": np.asarray(L0_gnn_att_a).reshape(1, DIM),
        "W_ff1": L0_gnn_W_ff1, "W_ff2": L0_gnn_W_ff2, "wr": np.asarray(L0_ffn_wr).reshape(1, DIM),
        "br": np.asarray(L0_ffn_br).reshape(1, 1), "w1": L0_ffn_w1, "b1": L0_ffn_b1, "w2": L0_ffn_w2,
        "b2": np.asarray(L0_ffn_b2).reshape(1, DIM),
    }
    arrays = {name: np.ascontiguousarray(a) for name, a in arrays.items()}
    nc = bacc.Bacc("TRN2", target_bir_lowering=False, num_devices=1)
    args = [nc.dram_tensor(name, a.shape, mybir.dt.from_np(a.dtype), kind="ExternalInput").ap()
            for name, a in arrays.items()]
    out = nc.dram_tensor("out", (N, DIM), F32, kind="ExternalOutput").ap()
    build(nc, *args, out)
    return run_bass_kernel_spmd(nc, [arrays], core_ids=[0]).results[0]["out"]
```

```python
from contextlib import ExitStack

import concourse.bass as bass
from concourse import mybir

P = 128
DIM = 256
CH = DIM // P
EDGE_DIM = 64
HEADS = 4
HEAD_DIM = DIM // HEADS
HOPS = 3
GAMMA = 0.5
FF = 512
FFJ = FF // P
HID = 1024
HJ = HID // P
EPS = 1e-5
N = 6250
WINDOWS = -(-N // P)
NP = WINDOWS * P
TAIL = N - (WINDOWS - 1) * P
E = 106250
TILES_IN_GROUP = 4
GROUP = TILES_IN_GROUP * P
RING = 4
UNROLL = 2 * RING
GROUPS = -(-E // (GROUP * UNROLL)) * UNROLL
TILES = GROUPS * TILES_IN_GROUP
EP = TILES * P
VISITS = GROUPS + WINDOWS - 1
SELECTED = N // 2 - 1
WCOL = DIM + 1
SEVEN = 7
assert WINDOWS % SEVEN == 0
BLOCK = 4
BLOCKS = WINDOWS // BLOCK
LOWEST = -3.0e38

ALU = mybir.AluOpType
ACT = mybir.ActivationFunctionType
AX = mybir.AxisListType.X
F32 = mybir.dt.float32
I32 = mybir.dt.int32


def build(nc, x, src, dst, group_last, edges, W_x, W_e, att, W_ff1, W_ff2, wr, br, w1, b1, w2, b2, out):
    with ExitStack() as ctx:
        def sb(name, shape, dt=F32):
            return ctx.enter_context(nc.sbuf_tensor(name, shape, dt))

        def sem(name):
            return ctx.enter_context(nc.semaphore(name))

        tables = [nc.dram_tensor(f"hop_table{k}", (NP, DIM), F32, kind="Internal").ap() for k in range(HOPS)]

        even = sb("even", [P, WINDOWS, DIM])
        odd = sb("odd", [P, WINDOWS, WCOL])
        neighbours = sb("neighbours", [P, RING, TILES_IN_GROUP, DIM])
        edge_ring = sb("edge_ring", [P, RING, 2, P])
        sums = sb("sums", [P, 2, TILES_IN_GROUP, DIM])
        messages = sb("messages", [P, 2, TILES_IN_GROUP, WCOL])
        onehot = sb("onehot", [P, 3, TILES_IN_GROUP, P])
        src_all = sb("src_all", [P, TILES], I32)
        src_now = sb("src_now", [P, 2, RING * TILES_IN_GROUP], I32)
        dst_int = sb("dst_int", [P, TILES], I32)
        dst_all = sb("dst_all", [P, TILES])
        last_dst = sb("last_dst", [1, GROUPS], I32)
        first_window = sb("first_window", [1, GROUPS + 1], I32)
        node_row = sb("node_row", [P, P])
        window_base = sb("window_base", [P, WINDOWS])
        ident = sb("ident", [P, P])
        zeros = sb("zeros", [P, DIM])
        ones = sb("ones", [P, P])
        below = sb("below", [P, P])
        wx_sb = sb("wx_sb", [P, CH, DIM])
        we_sb = sb("we_sb", [P, DIM])
        wff1_sb = sb("wff1_sb", [P, CH, FF])
        wff2_sb = sb("wff2_sb", [P, FFJ, DIM])
        w1_sb = sb("w1_sb", [P, CH, HID])
        w2_sb = sb("w2_sb", [P, HJ, DIM])
        b1_sb = sb("b1_sb", [P, HJ])
        rows = sb("rows", [1, 3 * DIM + 1])
        rows_all = sb("rows_all", [P, 3 * DIM + 1])
        att_all = rows_all[:, 0:DIM]
        wr_all = rows_all[:, DIM:2 * DIM]
        b2_all = rows_all[:, 2 * DIM:3 * DIM]
        br_all = rows_all[:, 3 * DIM:3 * DIM + 1]
        half_degree = sb("half_degree", [P, WINDOWS])
        stats = sb("stats", [P, 6 * SEVEN])
        aggregates = sb("aggregates", [P, 2 * SEVEN])
        roots_plus = sb("roots_plus", [P, WINDOWS])
        minus_means = sb("minus_means", [P, WINDOWS])
        moment = sb("moment", [P, 2 * WINDOWS])
        roots = sb("roots", [P, WINDOWS])
        root_t = sb("root_t", [P, WINDOWS])
        root_v = sb("root_v", [P, WINDOWS])
        ring_flat = neighbours[:].rearrange("p r t d -> p (r t d)")
        sums_flat = sums[:].rearrange("p r t d -> p (r t d)")
        normal = [ring_flat[:, b * DIM:(b + 1) * DIM] for b in range(2)]
        normal_T = [ring_flat[:, (2 + b) * DIM:(3 + b) * DIM] for b in range(2)]

        e_ps = ctx.enter_context(nc.psum_tensor("e_ps", [P, 2, TILES_IN_GROUP * DIM], F32))
        sum_ps = ctx.enter_context(nc.psum_tensor("sum_ps", [P, 2, 512], F32))
        more_ps = ctx.enter_context(nc.psum_tensor("more_ps", [P, 2, 512], F32))
        visit_ps = [sum_ps[:, 0], sum_ps[:, 1], more_ps[:, 0]]
        EXTRA = 2

        x_landed = [sem(f"x_landed{part}") for part in range(SEVEN)]
        tables_landed = sem("tables_landed")
        weights_landed = sem("weights_landed")
        rows_landed = sem("rows_landed")
        consts_made = sem("consts_made")
        CONSTS = 11
        rows_made = sem("rows_made")
        dve_step = sem("dve_step")
        normal_made = sem("normal_made")
        normal_turned = sem("normal_turned")
        normal_T_made = sem("normal_T_made")
        h0_summed = sem("h0_summed")
        h0_made = sem("h0_made")
        cleared = sem("cleared")
        published = sem("published")
        edge_landed = [sem(f"edge_landed{r}") for r in range(RING)]
        gathered = [sem(f"gathered{r}") for r in range(RING)]
        src_staged = sem("src_staged")
        edge_multiplied = sem("edge_multiplied")
        added = sem("added")
        relued = sem("relued")
        onehot_ready = sem("onehot_ready")
        scattered = sem("scattered")
        flushed = sem("flushed")
        window_done = sem("window_done")
        hop_started = sem("hop_started")

        block = ctx.enter_context(nc.Block())

        def rolled(eng, n, body, head):
            for i in range(head):
                body(i)
            with eng.Fori(head, n) as i:
                body(i)

        def stage(fn, w):
            if not isinstance(w, int) or 0 <= w < WINDOWS:
                fn(w)

        def after(eng, s, count):
            if not (isinstance(count, int) and count <= 0):
                eng.wait_ge(s, count)

        def next_window(w):
            return (w + 1).with_bounds(min_val=1, max_val=WINDOWS - 1)

        def load_windows(eng, it):
            return nc.values_load_multi_w_load_instructions(
                first_window[:, bass.ds(it * UNROLL, UNROLL + 1)], engines=(eng.engine,), min_val=0,
                max_val=WINDOWS - 1)[1]

        def window(ap, w, width, n):
            return ap[:, bass.ds(w * width, n)]

        even_flat = even[:].rearrange("p w d -> p (w d)")
        odd_flat = odd[:].rearrange("p w d -> p (w d)")

        def state(k, w, n=DIM):
            return window(even_flat, w, DIM, n) if k % 2 == 0 else window(odd_flat, w, WCOL, n)

        def early(w, k, first=0, n=DIM):
            return early_flat[:, bass.ds(w % 2 * (2 * DIM) + (k * DIM + first), n)]

        def dram_rows(t, w):
            return t[bass.ds(w * P, P), :]

        turned_ps = [e_ps[:, 0, b * 512:b * 512 + DIM] for b in range(2)]
        h0_ps = [e_ps[:, 1, b * 512:b * 512 + DIM] for b in range(2)]

        early_flat = ring_flat[:, 0:4 * DIM]
        x_row = ring_flat[:, 4 * DIM:5 * DIM]
        query = ring_flat[:, 5 * DIM:8 * DIM]
        weighed = ring_flat[:, 8 * DIM:12 * DIM]
        attended = ring_flat[:, 12 * DIM:13 * DIM]
        attended_T = ring_flat[:, 13 * DIM:14 * DIM]
        xln = ring_flat[:, 14 * DIM:15 * DIM]
        tanhs = sums_flat[:, 0:4 * DIM]
        scaled = sums_flat[:, 4 * DIM:8 * DIM]
        messages_flat = messages[:].rearrange("p r t d -> p (r t d)")
        hidden_T = messages_flat[:, 0:FF]
        ffsum = messages_flat[:, FF:FF + DIM]
        halves = messages_flat[:, FF + 4 * DIM:FF + 6 * DIM]
        x1 = messages_flat[:, FF + DIM:FF + 2 * DIM]
        x1_ln = messages_flat[:, FF + 2 * DIM:FF + 3 * DIM]
        product = messages_flat[:, FF + 3 * DIM:FF + 4 * DIM]
        score = sb("score", [P, 4 * HEADS])
        maxs = sb("maxs", [P, HEADS])
        less = sb("less", [P, 4 * HEADS])
        exps = sb("exps", [P, 4 * HEADS])
        denominator = sb("denominator", [P, 2 * HEADS])
        alpha = sb("alpha", [P, 4 * HEADS])
        mlp_weight = sb("mlp_weight", [P, WINDOWS])
        attended_T_ps = e_ps[:, 0, 0:DIM]
        hidden_ps = e_ps[:, 0, 512:1024]
        ffsum_ps = e_ps[:, 1, 0:DIM]
        x1_T_ps = e_ps[:, 1, 512:512 + DIM]

        early_landed = sem("early_landed")
        x_row_landed = sem("x_row_landed")
        xln_made = sem("xln_made")
        router_made = sem("router_made")
        queries_made = sem("queries_made")
        tanhs_made = sem("tanhs_made")
        less_made = sem("less_made")
        exps_made = sem("exps_made")
        alpha_made = sem("alpha_made")
        scaled_made = sem("scaled_made")
        attended_made = sem("attended_made")
        attended_turned = sem("attended_turned")
        attended_T_made = sem("attended_T_made")
        hidden_summed = sem("hidden_summed")
        hidden_made = sem("hidden_made")
        ff_summed = sem("ff_summed")
        x1_made = sem("x1_made")
        x1_ln_made = sem("x1_ln_made")
        x1_turned = sem("x1_turned")
        x1_T_made = sem("x1_T_made")
        search = sb("search", [P, 16])
        found = sb("found", [P, WINDOWS])
        equals = sb("equals", [P, WINDOWS])
        prefix = sb("prefix", [P, WINDOWS])
        chosen = sb("chosen", [P, WINDOWS])
        counts_made = sem("counts_made")
        totals_made = sem("totals_made")
        chosen_made = sem("chosen_made")
        hidden2_T = ring_flat[:, 0:HJ * BLOCK * P].rearrange("p (j n) -> p j n", j=HJ)
        biased = sums_flat[:, 0:2 * DIM]
        result = sums_flat[:, 4 * DIM:8 * DIM].rearrange("p (v d) -> p v d", v=BLOCK)
        mlp1_summed = sem("mlp1_summed")
        gelu_made = sem("gelu_made")
        biased_made = sem("biased_made")
        window_table_made = sem("window_table_made")
        mlp2_summed = sem("mlp2_summed")
        result_made = sem("result_made")
        out_stored = sem("out_stored")
        mlp1_ps = more_ps
        mlp2_ps = sum_ps

        @block.sync
        def _(sp):
            for part in range(SEVEN - 1):
                first = part * (WINDOWS // SEVEN)
                last = first + WINDOWS // SEVEN
                sp.dma_start(odd[:, first:last, 0:DIM],
                             x[first * P:last * P, :].rearrange("(w p) d -> p w d", p=P)).then_inc(x_landed[part], 16)
            sp.dma_start(odd[:, last:WINDOWS - 1, 0:DIM],
                         x[last * P:(WINDOWS - 1) * P, :].rearrange("(w p) d -> p w d", p=P)
                         ).then_inc(x_landed[SEVEN - 1], 16)
            sp.wait_ge(consts_made, 1)
            sp.dma_start(odd[0:TAIL, WINDOWS - 1, 0:DIM], x[(WINDOWS - 1) * P:N, :]).then_inc(x_landed[SEVEN - 1], 16)
            sp.dma_start(wx_sb[:], W_x.rearrange("(c p) n -> p c n", p=P)).then_inc(weights_landed, 16)
            for h in range(2):
                sp.dma_start(we_sb[h * EDGE_DIM:(h + 1) * EDGE_DIM, :], W_e).then_inc(weights_landed, 16)
            sp.dma_start(src_all[:], src).then_inc(tables_landed, 16)
            sp.dma_start(dst_int[:], dst).then_inc(tables_landed, 16)
            sp.dma_start(last_dst[:], group_last).then_inc(tables_landed, 16)
            sp.dma_start(wff1_sb[:], W_ff1.rearrange("(c p) n -> p c n", p=P)).then_inc(weights_landed, 16)
            sp.dma_start(wff2_sb[:], W_ff2.rearrange("(c p) n -> p c n", p=P)).then_inc(weights_landed, 16)
            sp.dma_start(w1_sb[:], w1.rearrange("(c p) n -> p c n", p=P)).then_inc(weights_landed, 16)
            sp.dma_start(w2_sb[:], w2.rearrange("(c p) n -> p c n", p=P)).then_inc(weights_landed, 16)
            with nc.allow_non_contiguous_dma(reason="1024 numbers, once"):
                sp.dma_start(b1_sb[:], b1.rearrange("(j p) -> p j", p=P)).then_inc(weights_landed, 16)
            sp.dma_start(rows[:, 0:DIM], att).then_inc(rows_landed, 16)
            sp.dma_start(rows[:, DIM:2 * DIM], wr).then_inc(rows_landed, 16)
            sp.dma_start(rows[:, 2 * DIM:3 * DIM], b2).then_inc(rows_landed, 16)
            sp.dma_start(rows[:, 3 * DIM:3 * DIM + 1], br).then_inc(rows_landed, 16)

            with sp.Fori(0, WINDOWS) as w:
                sp.wait_ge(h0_made, w + 1)
                sp.dma_start(dram_rows(tables[0], w), state(0, w)).then_inc(published, 16)

            for k in range(HOPS - 1):
                with sp.Fori(0, WINDOWS) as w:
                    sp.wait_ge(window_done, w + (k * WINDOWS + 1))
                    sp.dma_start(dram_rows(tables[k + 1], w), state(k + 1, w)).then_inc(published, 16)

            sp.wait_ge(published, 16 * WINDOWS * HOPS)
            sp.wait_ge(added, RING + HOPS * GROUPS)

            def load(w):
                after(sp, scaled_made, w - 1)
                sp.nop(nofuse=True)
                after(sp, early_landed, w * 32)
                sp.nop(nofuse=True)
                for k in range(2):
                    sp.dma_start(early(w, k), dram_rows(tables[k], w)).then_inc(early_landed, 16)
                after(sp, xln_made, w)
                sp.nop(nofuse=True)
                if isinstance(w, int) and w == WINDOWS - 1:
                    sp.dma_start(x_row[0:TAIL, :], x[w * P:N, :]).then_inc(x_row_landed, 16)
                else:
                    sp.dma_start(x_row, dram_rows(x, w)).then_inc(x_row_landed, 16)

            rolled(sp, WINDOWS - 1, load, 2)
            load(WINDOWS - 1)

            with sp.Fori(0, BLOCKS) as b:
                sp.wait_ge(result_made, b * BLOCK + BLOCK)
                sp.dma_start(out[bass.ds(b * (BLOCK * P), BLOCK * P), :].rearrange("(v p) d -> p v d", p=P),
                             result).then_inc(out_stored, 16)
            sp.wait_ge(result_made, WINDOWS)
            sp.dma_start(out[(WINDOWS - 1) * P:N, :], result[0:TAIL, 0, :]).then_inc(out_stored, 16)
            sp.wait_ge(out_stored, 16 * (BLOCKS + 1))

        @block.gpsimd
        def _(pool):
            nc.gpsimd.memset(odd[:, WINDOWS - 1, :], 0.0).then_inc(consts_made, 1)
            nc.gpsimd.memset(ident[:], 0.0).then_inc(consts_made, 1)
            nc.gpsimd.memset(below[:], 1.0).then_inc(consts_made, 1)
            pool.wait_ge(consts_made, 3)
            nc.gpsimd.affine_select(out=ident[:], in_=ident[:], compare_op=ALU.not_equal, fill=1.0, base=0,
                                    pattern=[[-1, P]], channel_multiplier=1).then_inc(consts_made, 1)
            nc.gpsimd.affine_select(out=below[:], in_=below[:], compare_op=ALU.is_gt, fill=0.0, base=0,
                                    pattern=[[1, P]], channel_multiplier=-1).then_inc(consts_made, 1)
            nc.gpsimd.iota(node_row[:], pattern=[[1, P]], base=0, channel_multiplier=0,
                           allow_small_or_imprecise_dtypes=True).then_inc(consts_made, 1)
            nc.gpsimd.iota(window_base[:], pattern=[[P, WINDOWS]], base=0, channel_multiplier=0,
                           allow_small_or_imprecise_dtypes=True).then_inc(consts_made, 1)
            nc.gpsimd.memset(messages[:], 1.0).then_inc(consts_made, 1)
            nc.gpsimd.memset(first_window[:, 0:1], 0).then_inc(consts_made, 1)
            nc.gpsimd.memset(ones[:], 1.0).then_inc(consts_made, 1)
            nc.gpsimd.memset(zeros[:], 0.0).then_inc(consts_made, 1)
            pool.wait_ge(rows_landed, 64)
            nc.gpsimd.partition_broadcast(rows_all[:], rows[:], channels=P).then_inc(rows_made, 1)
            with pool.Fori(0, WINDOWS) as w:
                pool.wait_ge(normal_made, w + 1)
                pool.nop(nofuse=True)
                nc.gpsimd.tensor_copy(state(1, w), zeros[:]).then_inc(cleared, 1)
            pool.wait_ge(tables_landed, 48)
            for k in range(HOPS):
                pool.wait_ge(published, 16 * WINDOWS * (k + 1))
                if k == 0:
                    pool.wait_ge(h0_summed, WINDOWS)
                with pool.Fori(0, GROUPS // UNROLL) as it:
                    for u in range(UNROLL):
                        r = u % RING
                        g = it * UNROLL + u + k * GROUPS
                        half = u // RING
                        pool.wait_ge(added, g + 1)
                        if r == 0:
                            pool.nop(nofuse=True)
                            cols = bass.ds(it * (UNROLL * TILES_IN_GROUP) + half * RING * TILES_IN_GROUP,
                                           RING * TILES_IN_GROUP)
                            nc.gpsimd.tensor_copy(src_now[:, half, :], src_all[:, cols]).then_inc(src_staged, 1)
                            pool.wait_ge(src_staged, it * 2 + (half + 1 + 2 * k * (GROUPS // UNROLL)))
                        pool.nop(nofuse=True)
                        for t in range(TILES_IN_GROUP):
                            i = r * TILES_IN_GROUP + t
                            nc.gpsimd.indirect_dma_start(
                                out=neighbours[:, r, t, :], out_offset=None, in_=tables[k],
                                in_offset=bass.IndirectOffsetOnAxis(ap=src_now[:, half, i:i + 1], axis=0),
                            ).then_inc(gathered[r], 16)

        @block.scalar
        def _(act):
            def turn_copies(i):
                for u in range(SEVEN):
                    w = i * SEVEN + u
                    act.wait_ge(normal_turned, w + 1)
                    after(act, h0_summed, w - (0 if u == 0 else 1))
                    nc.scalar.copy(normal_T[u % 2], turned_ps[u % 2]).then_inc(normal_T_made, 1)

            rolled(act, WINDOWS // SEVEN, turn_copies, 1)

            def load_edges(k, g, u):
                act.wait_ge(edge_multiplied, g + (k * GROUPS + 1))
                act.dma_start(edge_ring[:, u % RING],
                              edges[:, bass.ds(g * 2 * P, 2 * P)].rearrange("p (j e) -> p j e", j=2)
                              ).then_inc(edge_landed[u % RING], 16)

            act.sem_inc(relued, 2)
            for k in range(HOPS):
                load_edges(k, 0, 0)
                load_edges(k, 1, 1)

                def rectify(it, last):
                    for u in range(RING):
                        g = it * RING + u
                        if not last or u + 2 < RING:
                            load_edges(k, g + 2, u + 2)
                        act.wait_ge(added, g + (RING + k * GROUPS + 1))
                        if k == 0 and u < 2:
                            act.wait_ge(consts_made, CONSTS)
                        nc.scalar.activation(messages[:, u % 2, :, 0:DIM], sums[:, u % 2], ACT.Relu).then_inc(relued, 1)

                with act.Fori(0, GROUPS // RING - 1) as it:
                    rectify(it, False)
                rectify(GROUPS // RING - 1, True)

            def tanh_stage(w):
                act.wait_ge(early_landed, w * 32 + 32)
                act.wait_ge(queries_made, w + 1)
                act.nop(nofuse=True)
                nc.scalar.activation(tanhs[:, 0:DIM], early(w, 0), ACT.Tanh, scale=2.0)
                nc.scalar.activation(tanhs[:, DIM:4 * DIM], query, ACT.Tanh).then_inc(tanhs_made, 1)

            def turned_stage(w):
                act.wait_ge(attended_turned, w + 1)
                nc.scalar.copy(attended_T, attended_T_ps).then_inc(attended_T_made, 1)
                act.wait_ge(x_row_landed, w * 16 + 16)
                after(act, x1_made, w)
                act.nop(nofuse=True)
                nc.scalar.activation(xln, x_row, ACT.Identity, scale=roots_plus[:, bass.ds(w, 1)],
                                     bias=minus_means[:, bass.ds(w, 1)]).then_inc(xln_made, 1)

            def exp_stage(w):
                act.wait_ge(less_made, w + 1)
                nc.scalar.activation(exps[:], less[:], ACT.Exp).then_inc(exps_made, 1)

            def hidden_stage(w):
                act.wait_ge(hidden_summed, w + 1)
                nc.scalar.activation(hidden_T, hidden_ps, ACT.Relu).then_inc(hidden_made, 1)

            def scale_stage(w):
                act.wait_ge(alpha_made, w + 1)
                after(act, attended_made, w)
                act.nop(nofuse=True)
                for k in range(HOPS + 1):
                    for h in range(HEADS):
                        source = (early(w, k, h * HEAD_DIM, HEAD_DIM) if k < 2
                                  else state(k, w)[:, h * HEAD_DIM:(h + 1) * HEAD_DIM])
                        last = nc.scalar.activation(
                            scaled[:, k * DIM + h * HEAD_DIM:k * DIM + (h + 1) * HEAD_DIM], source, ACT.Copy,
                            scale=alpha[:, k * HEADS + h:k * HEADS + h + 1])
                last.then_inc(scaled_made, 1)

            def turn_x1(w):
                act.wait_ge(x1_turned, w + 1)
                act.nop(nofuse=True)
                nc.scalar.copy(state(0, w), x1_T_ps).then_inc(x1_T_made, 1)

            def attend_step(i):
                stage(tanh_stage, i)
                stage(turn_x1, i - 2)
                stage(turned_stage, i - 1)
                stage(exp_stage, i)
                stage(hidden_stage, i - 1)
                stage(scale_stage, i)

            rolled(act, WINDOWS, attend_step, 3)
            attend_step(WINDOWS)
            attend_step(WINDOWS + 1)

            def gelus(b, width):
                for j in range(HJ):
                    act.wait_ge(mlp1_summed, b * HJ + j + 1)
                    if j == 0:
                        after(act, mlp2_summed, b * BLOCK)
                    nc.scalar.activation(hidden2_T[:, j, 0:width], mlp1_ps[:, j % 2, 0:width], ACT.Gelu_apprx_tanh,
                                         bias=b1_sb[:, j:j + 1]).then_inc(gelu_made, 1)

            rolled(act, BLOCKS, lambda b: gelus(b, BLOCK * P), 1)
            gelus(BLOCKS, P)

        @block.vector
        def _(dve):
            chain = [0, 0]

            def link(ins):
                ins.then_inc(dve_step, 1)
                chain[1] += 1
                dve.wait_ge(dve_step, chain[0] + chain[1])

            def rolled_links(n, body, head):
                for i in range(head):
                    before = chain[1]
                    body(i)
                each, before = chain[1] - before, chain[1]
                with dve.Fori(head, n) as i:
                    chain[:] = [(i - head) * each, before]
                    body(i)
                chain[:] = [0, before + each * (n - head)]

            dve.sem_inc(added, RING)
            dve.sem_inc(flushed, 1)
            dve.wait_ge(consts_made, CONSTS)
            dve.wait_ge(tables_landed, 48)
            link(nc.vector.tensor_copy(dst_all[:], dst_int[:]))
            nc.vector.tensor_single_scalar(first_window[:, 1:GROUPS + 1], last_dst[:], P.bit_length() - 1,
                                           op=ALU.arith_shift_right).then_inc(window_table_made, 1)
            dve.wait_ge(window_table_made, 1)

            def rsqrt(root, value, t, v):
                link(nc.vector.tensor_scalar(v, value, EPS, None, ALU.add))
                link(nc.vector.tensor_single_scalar(t.bitcast(I32), v.bitcast(I32), 1, op=ALU.logical_shift_right))
                link(nc.vector.tensor_scalar(root.bitcast(I32), t.bitcast(I32), -1.0, float(0x5F3759DF),
                                             ALU.mult, ALU.add))
                link(nc.vector.tensor_tensor(t, root, root, ALU.mult))
                for i in range(3):
                    link(nc.vector.tensor_tensor(t, t, v, ALU.mult))
                    link(nc.vector.tensor_scalar(t, t, -0.5, 1.5, ALU.mult, ALU.add))
                    link(nc.vector.tensor_tensor(root, root, t, ALU.mult))
                    if i < 2:
                        link(nc.vector.tensor_tensor(t, root, root, ALU.mult))

            def moments(i):
                for u in range(SEVEN):
                    ins = nc.vector.bn_stats(stats[:, u * 6:u * 6 + 6], state(1, i * SEVEN + u))
                link(ins)
                for u in range(SEVEN):
                    ins = nc.vector.bn_aggr(aggregates[:, 2 * u:2 * u + 2], stats[:, u * 6:u * 6 + 6])
                link(ins)
                link(nc.vector.tensor_copy(moment[:, i * 2 * SEVEN:(i + 1) * 2 * SEVEN], aggregates[:]))

            for part in range(SEVEN):
                dve.wait_ge(x_landed[part], 32 if part == SEVEN - 1 else 16)
                moments(part)
            mean, variance = (moment[:].rearrange("p (w two) -> p w two", two=2)[:, :, c] for c in range(2))
            rsqrt(roots[:], variance, root_t[:], root_v[:])
            link(nc.vector.tensor_scalar(roots_plus[:], roots[:], 1.0, None, ALU.add))
            link(nc.vector.scalar_tensor_tensor(out=minus_means[:], in0=mean, scalar=-1.0, in1=roots[:],
                                                op0=ALU.mult, op1=ALU.mult))

            def normalise(w, u):
                after(dve, normal_turned, w - (0 if u == 0 else 1))
                nc.vector.tensor_scalar(normal[u % 2], state(1, w), moment[:, bass.ds(w * 2, 1)],
                                        roots[:, bass.ds(w, 1)], ALU.subtract, ALU.mult).then_inc(normal_made, 1)

            def copy_h0(w, u):
                dve.wait_ge(h0_summed, w + 1)
                nc.vector.tensor_scalar(state(0, w), h0_ps[u % 2], 1.0, None, ALU.mult).then_inc(h0_made, 1)

            def node_steps(i):
                for u in range(SEVEN):
                    normalise(i * SEVEN + u, u)
                    for v in (u - 2,):
                        if v >= 0:
                            copy_h0(i * SEVEN + v, v)
                for v in (SEVEN - 2, SEVEN - 1):
                    copy_h0(i * SEVEN + v, v)

            rolled(dve, WINDOWS // SEVEN, node_steps, 1)
            dve.wait_ge(cleared, WINDOWS)
            link(nc.vector.memset(odd[:, :, DIM:WCOL], 0.0))

            for k in range(HOPS):
                if k == 1:
                    link(nc.vector.tensor_scalar(half_degree[:], odd[:, :, DIM:WCOL].rearrange("p w o -> p (w o)"),
                                                 -GAMMA, None, ALU.mult))
                if k:
                    dve.wait_ge(published, 16 * WINDOWS * k)
                    with dve.Fori(0, WINDOWS) as w:
                        nc.vector.tensor_scalar(state(k + 1, w), state(k + 1, w), half_degree[:, bass.ds(w, 1)], None,
                                                ALU.mult).then_inc(hop_started, 1)
                    dve.wait_ge(hop_started, k * WINDOWS)
                width = WCOL if k == 0 else DIM

                def add(it, u):
                    r = u % RING
                    use = it * (UNROLL // RING) + u // RING + k * (GROUPS // RING)
                    dve.wait_ge(edge_multiplied, it * UNROLL + (u + k * GROUPS + RING + 1))
                    dve.wait_ge(relued, it * UNROLL + (u + k * GROUPS + 1))
                    dve.wait_ge(gathered[r], (use + 1) * (16 * TILES_IN_GROUP))
                    nc.vector.tensor_tensor(sums[:, u % 2].rearrange("p t d -> p (t d)"), e_ps[:, u % 2, :],
                                            neighbours[:, r].rearrange("p t d -> p (t d)"), ALU.add).then_inc(added, 1)

                def make_onehot(it, u, w, slot):
                    d = dst_all[:, bass.ds(it * (UNROLL * TILES_IN_GROUP) + u * TILES_IN_GROUP, TILES_IN_GROUP)]
                    nc.vector.scalar_tensor_tensor(
                        out=onehot[:, slot],
                        in0=node_row[:].unsqueeze(1).broadcast_to([P, TILES_IN_GROUP, P]),
                        scalar=window_base[:, bass.ds(w, 1)],
                        in1=d.unsqueeze(2).broadcast_to([P, TILES_IN_GROUP, P]),
                        op0=ALU.add, op1=ALU.is_equal).then_inc(onehot_ready, 1)

                def flush(it, u, w, slot):
                    visit = it * UNROLL + w + (u + k * VISITS)
                    dve.wait_ge(scattered, visit + 1)
                    dve.wait_ge(flushed, visit + 1)
                    acc = state(k + 1, w, width)
                    nc.vector.tensor_tensor(acc, visit_ps[slot][:, 0:width], acc, ALU.add).then_inc(flushed, 1)

                def leave(it, u, w):
                    dve.wait_ge(flushed, it * UNROLL + w + (u + k * VISITS + 1))
                    dve.nop(nofuse=True)
                    nc.vector.engine_nop().then_inc(window_done, 1)

                def walk(it, last):
                    ws = load_windows(dve, it)
                    for u in range(UNROLL):
                        make_onehot(it, u, ws[u], u % 2)
                        with dve.If(ws[u] < ws[u + 1]):
                            make_onehot(it, u, next_window(ws[u]), EXTRA)
                        if not last or u + 1 < UNROLL:
                            add(it, u + 1)
                        flush(it, u, ws[u], u % 2)
                        with dve.If(ws[u] < ws[u + 1]):
                            leave(it, u, next_window(ws[u]))
                            flush(it, u, next_window(ws[u]), EXTRA)
                            with dve.If(ws[u] + 1 < ws[u + 1]):
                                with dve.Fori(ws[u] + 2, ws[u + 1] + 1) as w:
                                    leave(it, u, w)
                                    make_onehot(it, u, w, EXTRA)
                                    flush(it, u, w, EXTRA)

                add(0, 0)
                with dve.Fori(0, GROUPS // UNROLL - 1) as it:
                    walk(it, False)
                walk(GROUPS // UNROLL - 1, True)
                dve.wait_ge(flushed, 1 + (k + 1) * VISITS)
                nc.vector.engine_nop().then_inc(window_done, 1)

            def query_stage(w):
                dve.wait_ge(early_landed, w * 32 + 32)
                after(dve, tanhs_made, w)
                dve.nop(nofuse=True)
                for k in range(1, HOPS + 1):
                    h = early(w, k) if k < 2 else state(k, w)
                    last = nc.vector.tensor_tensor(query[:, (k - 1) * DIM:k * DIM], h, early(w, 0), ALU.add)
                last.then_inc(queries_made, 1)

            def attended_stage(w):
                dve.wait_ge(scaled_made, w + 1)
                link(nc.vector.tensor_tensor(halves, scaled[:, 0:2 * DIM], scaled[:, 2 * DIM:4 * DIM], ALU.add))
                nc.vector.tensor_tensor(attended, halves[:, 0:DIM], halves[:, DIM:2 * DIM],
                                        ALU.add).then_inc(attended_made, 1)

            def score_stage(w):
                dve.wait_ge(tanhs_made, w + 1)
                link(nc.vector.tensor_tensor(weighed.rearrange("p (k d) -> p k d", d=DIM),
                                             tanhs.rearrange("p (k d) -> p k d", d=DIM),
                                             att_all.unsqueeze(1).broadcast_to([P, 4, DIM]), ALU.mult))
                link(nc.vector.tensor_reduce(score[:], weighed.rearrange("p (s d) -> p s d", d=HEAD_DIM), AX, ALU.add))
                link(nc.vector.tensor_reduce(maxs[:], score[:].rearrange("p (k h) -> p h k", h=HEADS), AX, ALU.max))
                nc.vector.tensor_tensor(less[:].rearrange("p (k h) -> p k h", h=HEADS),
                                        score[:].rearrange("p (k h) -> p k h", h=HEADS),
                                        maxs[:].unsqueeze(1).broadcast_to([P, 4, HEADS]),
                                        ALU.subtract).then_inc(less_made, 1)

            def alpha_stage(w):
                dve.wait_ge(exps_made, w + 1)
                link(nc.vector.tensor_reduce(denominator[:, 0:HEADS], exps[:].rearrange("p (k h) -> p h k", h=HEADS),
                                             AX, ALU.add))
                link(nc.vector.reciprocal(denominator[:, HEADS:2 * HEADS], denominator[:, 0:HEADS]))
                nc.vector.tensor_tensor(alpha[:].rearrange("p (k h) -> p k h", h=HEADS),
                                        exps[:].rearrange("p (k h) -> p k h", h=HEADS),
                                        denominator[:, HEADS:2 * HEADS].unsqueeze(1).broadcast_to([P, 4, HEADS]),
                                        ALU.mult).then_inc(alpha_made, 1)

            def residual_stage(w):
                dve.wait_ge(ff_summed, w + 1)
                link(nc.vector.tensor_tensor(ffsum, ffsum_ps, attended, ALU.add))
                dve.wait_ge(xln_made, w + 1)
                nc.vector.scalar_tensor_tensor(out=x1, in0=ffsum, scalar=0.0, in1=xln, op0=ALU.max,
                                               op1=ALU.add).then_inc(x1_made, 1)
                dve.wait_ge(x1_made, w + 1)
                link(nc.vector.bn_stats(stats[:, 0:6], x1))
                dve.nop(nofuse=True)
                link(nc.vector.bn_aggr(aggregates[:, 0:2], stats[:, 0:6]))
                rsqrt(aggregates[:, 2:3], aggregates[:, 1:2], aggregates[:, 3:4], aggregates[:, 4:5])
                after(dve, x1_turned, w)
                nc.vector.tensor_scalar(x1_ln, x1, aggregates[:, 0:1], aggregates[:, 2:3],
                                        ALU.subtract, ALU.mult).then_inc(x1_ln_made, 1)
                dve.wait_ge(x1_ln_made, w + 1)
                link(nc.vector.tensor_tensor(product, x1_ln, wr_all, ALU.mult))
                nc.vector.tensor_reduce(mlp_weight[:, bass.ds(w, 1)], product, AX, ALU.add)
                nc.vector.tensor_tensor(state(3, w), x1, x1_ln, ALU.add).then_inc(router_made, 1)
                dve.wait_ge(router_made, w + 1)

            def attend_step(i):
                stage(query_stage, i)
                stage(attended_stage, i - 1)
                stage(score_stage, i)
                stage(alpha_stage, i)
                stage(residual_stage, i - 1)

            dve.wait_ge(rows_made, 1)
            rolled_links(WINDOWS, attend_step, 3)
            attend_step(WINDOWS)

            link(nc.vector.tensor_scalar(mlp_weight[:], mlp_weight[:], br_all, None, ALU.add))
            link(nc.vector.tensor_copy(found[:], mlp_weight[:]))
            link(nc.vector.tensor_reduce(search[:, 0:1], below[:, 0:TAIL], AX, ALU.add))
            link(nc.vector.tensor_scalar(search[:, 1:2], search[:, 0:1], 0.5, None, ALU.is_gt))
            last_w = found[:, WINDOWS - 1:WINDOWS]
            link(nc.vector.tensor_tensor(search[:, 1:2], search[:, 1:2], ident[:, TAIL - 1:TAIL], ALU.add))
            link(nc.vector.tensor_tensor(last_w, last_w, search[:, 1:2], ALU.mult))
            link(nc.vector.tensor_scalar(search[:, 2:3], search[:, 1:2], 1.0, -LOWEST, ALU.subtract, ALU.mult))
            link(nc.vector.tensor_tensor(last_w, last_w, search[:, 2:3], ALU.add))

            magnitude = search[:, 3:4].bitcast(I32)
            candidate = search[:, 4:5].bitcast(I32)
            bit = search[:, 5:6].bitcast(I32)
            signed = search[:, 6:7]
            count = search[:, 7:8]
            enough = search[:, 8:9]
            sign = search[:, 9:10]
            flip = search[:, 10:11]
            keep = search[:, 11:12]
            total_ps = more_ps[:, 0, 0:1]
            asked = [0]

            def total(against, op, values=found):
                link(nc.vector.tensor_scalar(equals[:], values[:], against, None, op))
                nc.vector.tensor_reduce(count, equals[:], AX, ALU.add).then_inc(counts_made, 1)
                asked[0] += 1
                dve.wait_ge(totals_made, asked[0])

            link(nc.vector.memset(search[:, 12:13], 0.0))
            total(search[:, 12:13], ALU.is_ge)
            link(nc.vector.tensor_scalar(enough, total_ps, float(SELECTED), None, ALU.is_ge))
            link(nc.vector.tensor_scalar(sign, enough, 2.0, -1.0, ALU.mult, ALU.add))
            link(nc.vector.tensor_scalar(flip, enough, -1.0, 1.0, ALU.mult, ALU.add))
            link(nc.vector.memset(magnitude, 0))
            link(nc.vector.memset(bit, 1 << 30))

            asked_before = asked[0]

            def try_bit(i):
                link(nc.vector.tensor_tensor(candidate, magnitude, bit, ALU.bitwise_or))
                link(nc.vector.tensor_tensor(signed, search[:, 4:5], sign, ALU.mult))
                link(nc.vector.tensor_scalar(equals[:], found[:], signed, None, ALU.is_ge))
                nc.vector.tensor_reduce(count, equals[:], AX, ALU.add).then_inc(counts_made, 1)
                dve.wait_ge(totals_made, i + (asked_before + 1))
                link(nc.vector.tensor_scalar(enough, total_ps, float(SELECTED), None, ALU.is_ge))
                link(nc.vector.tensor_tensor(keep, enough, flip, ALU.not_equal))
                link(nc.vector.tensor_scalar(search[:, 13:14].bitcast(I32), keep, -1.0, None, ALU.mult))
                link(nc.vector.tensor_tensor(search[:, 14:15].bitcast(I32), bit, search[:, 13:14].bitcast(I32),
                                             ALU.bitwise_and))
                link(nc.vector.tensor_tensor(magnitude, magnitude, search[:, 14:15].bitcast(I32), ALU.bitwise_or))
                link(nc.vector.tensor_single_scalar(bit, bit, 1, op=ALU.logical_shift_right))

            rolled_links(31, try_bit, 1)
            asked[0] += 31
            link(nc.vector.tensor_tensor(signed, search[:, 3:4], sign, ALU.mult))
            link(nc.vector.tensor_scalar(equals[:], found[:], signed, None, ALU.is_ge))
            link(nc.vector.tensor_scalar(prefix[:], found[:], signed, None, ALU.is_gt))
            link(nc.vector.tensor_tensor(chosen[:], equals[:], prefix[:], ALU.subtract))
            link(nc.vector.scalar_tensor_tensor(out=prefix[:], in0=chosen[:], scalar=flip, in1=prefix[:],
                                                op0=ALU.mult, op1=ALU.add))
            link(nc.vector.tensor_copy(chosen[:], prefix[:]))
            link(nc.vector.tensor_copy(search[:, 12:13].bitcast(I32), flip))
            link(nc.vector.tensor_scalar(search[:, 13:14].bitcast(I32), magnitude, 65535, None, ALU.bitwise_and))
            link(nc.vector.tensor_scalar(search[:, 14:15].bitcast(I32), magnitude, 16, None, ALU.logical_shift_right))
            link(nc.vector.tensor_tensor(search[:, 13:14].bitcast(I32), search[:, 13:14].bitcast(I32),
                                         search[:, 12:13].bitcast(I32), ALU.add))
            link(nc.vector.tensor_scalar(search[:, 12:13].bitcast(I32), search[:, 13:14].bitcast(I32), 16, None,
                                         ALU.logical_shift_right))
            link(nc.vector.tensor_tensor(search[:, 14:15].bitcast(I32), search[:, 14:15].bitcast(I32),
                                         search[:, 12:13].bitcast(I32), ALU.add))
            link(nc.vector.tensor_scalar(search[:, 14:15].bitcast(I32), search[:, 14:15].bitcast(I32), 16, None,
                                         ALU.logical_shift_left))
            link(nc.vector.tensor_scalar(search[:, 13:14].bitcast(I32), search[:, 13:14].bitcast(I32), 65535, None,
                                         ALU.bitwise_and))
            link(nc.vector.tensor_tensor(search[:, 15:16].bitcast(I32), search[:, 14:15].bitcast(I32),
                                         search[:, 13:14].bitcast(I32), ALU.bitwise_or))
            link(nc.vector.tensor_tensor(signed, search[:, 15:16], sign, ALU.mult))
            link(nc.vector.tensor_scalar(equals[:], found[:], signed, None, ALU.is_equal))
            nc.vector.tensor_reduce(count, chosen[:], AX, ALU.add).then_inc(counts_made, 1)
            asked[0] += 1
            dve.wait_ge(totals_made, asked[0])
            link(nc.vector.tensor_scalar(keep, total_ps, -1.0, float(SELECTED), ALU.mult, ALU.add))
            nc.vector.engine_nop().then_inc(chosen_made, 1)
            dve.wait_ge(chosen_made, 2)
            link(nc.vector.tensor_copy(prefix[:], more_ps[:, 1, 0:WINDOWS]))
            link(nc.vector.memset(half_degree[:], 1.0))
            link(nc.vector.tensor_tensor_scan(out=half_degree[:], data0=half_degree[:],
                                              data1=prefix[:], initial=0.0, op0=ALU.mult, op1=ALU.add))
            link(nc.vector.tensor_tensor(half_degree[:], half_degree[:], prefix[:], ALU.subtract))
            link(nc.vector.tensor_tensor(prefix[:], half_degree[:], more_ps[:, 1, WINDOWS:2 * WINDOWS], ALU.add))
            link(nc.vector.tensor_scalar(prefix[:], prefix[:], keep, None, ALU.is_lt))
            link(nc.vector.tensor_tensor(prefix[:], prefix[:], equals[:], ALU.mult))
            link(nc.vector.tensor_tensor(chosen[:], chosen[:], prefix[:], ALU.add))
            link(nc.vector.tensor_tensor(chosen[:], chosen[:], mlp_weight[:], ALU.mult))
            nc.vector.engine_nop().then_inc(chosen_made, 1)

            def results(b, v):
                n = b * BLOCK + v
                dve.wait_ge(mlp2_summed, n + 1)
                if v == 0:
                    after(dve, out_stored, b * 16)
                half = biased[:, (v % 2) * DIM:(v % 2 + 1) * DIM]
                nc.vector.tensor_tensor(half, mlp2_ps[:, v % 2, 0:DIM], b2_all, ALU.add).then_inc(biased_made, 1)
                dve.wait_ge(biased_made, n + 1)
                nc.vector.scalar_tensor_tensor(out=result[:, v, :], in0=half, scalar=chosen[:, bass.ds(n, 1)],
                                               in1=state(3, n), op0=ALU.mult, op1=ALU.add).then_inc(result_made, 1)

            def results_of_block(b):
                for v in range(BLOCK):
                    results(b, v)

            rolled(dve, BLOCKS, results_of_block, 1)
            results(BLOCKS, 0)

        @block.tensor
        def _(pe):
            pe.sem_inc(edge_multiplied, RING)
            pe.wait_ge(consts_made, CONSTS)
            pe.wait_ge(weights_landed, 16 * 8)

            def turn(w, u):
                pe.wait_ge(normal_made, w + 1)
                after(pe, normal_T_made, w - (0 if u == 0 else 1))
                for c in range(CH):
                    last = nc.tensor.transpose(turned_ps[u % 2][:, c * P:(c + 1) * P],
                                               normal[u % 2][:, c * P:(c + 1) * P], ident[:])
                last.then_inc(normal_turned, 1)

            def project(w, u):
                pe.wait_ge(normal_T_made, w + 1)
                after(pe, h0_made, w - (0 if u == 0 else 1))
                for c in range(CH):
                    last = nc.tensor.matmul(h0_ps[u % 2], normal_T[u % 2][:, c * P:(c + 1) * P], wx_sb[:, c, :],
                                            start=(c == 0), stop=(c == CH - 1))
                last.then_inc(h0_summed, 1)

            def node_steps(i):
                for u in range(SEVEN):
                    turn(i * SEVEN + u, u)
                    if u:
                        project(i * SEVEN + u - 1, u - 1)
                project(i * SEVEN + SEVEN - 1, SEVEN - 1)

            rolled(pe, WINDOWS // SEVEN, node_steps, 1)
            pe.wait_ge(h0_made, WINDOWS)

            for k in range(HOPS):
                width = WCOL if k == 0 else DIM

                def multiply_edges(it, u):
                    r = u % RING
                    use = it * (UNROLL // RING) + u // RING + k * (GROUPS // RING)
                    pe.wait_ge(edge_landed[r], (use + 1) * 16)
                    pe.wait_ge(added, it * UNROLL + (u + k * GROUPS + RING - 1))
                    for h in range(2):
                        part = slice(h * EDGE_DIM, (h + 1) * EDGE_DIM)
                        for j in range(2):
                            q = 2 * h + j
                            last = nc.tensor.matmul(e_ps[:, u % 2, q * DIM:(q + 1) * DIM], edge_ring[part, r, j, :],
                                                    we_sb[part, :], start=True, stop=True)
                    last.then_inc(edge_multiplied, 1)

                def scatter(it, u, w, slot):
                    pe.wait_ge(onehot_ready, it * UNROLL + w + (u + k * VISITS + 1))
                    for t in range(TILES_IN_GROUP):
                        last = nc.tensor.matmul(visit_ps[slot][:, 0:width], onehot[:, slot, t, :],
                                                messages[:, u % 2, t, 0:width], start=(t == 0),
                                                stop=(t == TILES_IN_GROUP - 1))
                    last.then_inc(scattered, 1)

                def walk(it, last):
                    ws = load_windows(pe, it)
                    for u in range(UNROLL):
                        if not last or u + 1 < UNROLL:
                            multiply_edges(it, u + 1)
                        pe.wait_ge(relued, it * UNROLL + (u + k * GROUPS + 3))
                        scatter(it, u, ws[u], u % 2)
                        with pe.If(ws[u] < ws[u + 1]):
                            scatter(it, u, next_window(ws[u]), EXTRA)
                            with pe.If(ws[u] + 1 < ws[u + 1]):
                                with pe.Fori(ws[u] + 2, ws[u + 1] + 1) as w:
                                    scatter(it, u, w, EXTRA)

                if k == 0:
                    pe.wait_ge(window_table_made, 1)
                multiply_edges(0, 0)
                with pe.Fori(0, GROUPS // UNROLL - 1) as it:
                    walk(it, False)
                walk(GROUPS // UNROLL - 1, True)

            def turn_attended(w):
                pe.wait_ge(attended_made, w + 1)
                for c in range(CH):
                    last = nc.tensor.transpose(attended_T_ps[:, c * P:(c + 1) * P], attended[:, c * P:(c + 1) * P],
                                               ident[:])
                last.then_inc(attended_turned, 1)

            def feed(w):
                pe.wait_ge(attended_T_made, w + 1)
                for j in range(FFJ):
                    for c in range(CH):
                        last = nc.tensor.matmul(hidden_ps[:, j * P:(j + 1) * P], wff1_sb[:, c, j * P:(j + 1) * P],
                                                attended_T[:, c * P:(c + 1) * P], start=(c == 0), stop=(c == CH - 1))
                last.then_inc(hidden_summed, 1)
                pe.wait_ge(hidden_made, w + 1)
                for j in range(FFJ):
                    last = nc.tensor.matmul(ffsum_ps, hidden_T[:, j * P:(j + 1) * P], wff2_sb[:, j, :],
                                            start=(j == 0), stop=(j == FFJ - 1))
                last.then_inc(ff_summed, 1)

            def turn_x1(w):
                pe.wait_ge(x1_ln_made, w + 1)
                after(pe, x1_T_made, w)
                for c in range(CH):
                    last = nc.tensor.transpose(x1_T_ps[:, c * P:(c + 1) * P], x1_ln[:, c * P:(c + 1) * P], ident[:])
                last.then_inc(x1_turned, 1)

            def attend_step(i):
                stage(turn_x1, i - 2)
                stage(turn_attended, i - 1)
                stage(feed, i - 1)

            rolled(pe, WINDOWS, attend_step, 3)
            attend_step(WINDOWS)
            attend_step(WINDOWS + 1)

            def sum_counts():
                nc.tensor.matmul(more_ps[:, 0, 0:1], ones[:], search[:, 7:8], start=True,
                                 stop=True).then_inc(totals_made, 1)

            pe.wait_ge(counts_made, 1)
            sum_counts()
            with pe.Fori(0, 31) as i:
                pe.wait_ge(counts_made, i + 2)
                sum_counts()
            pe.wait_ge(counts_made, 33)
            sum_counts()
            pe.wait_ge(chosen_made, 1)
            nc.tensor.matmul(more_ps[:, 1, 0:WINDOWS], ones[:], equals[:], start=True, stop=True)
            nc.tensor.matmul(more_ps[:, 1, WINDOWS:2 * WINDOWS], below[:], equals[:], start=True,
                             stop=True).then_inc(chosen_made, 1)
            pe.wait_ge(chosen_made, 3)
            pe.wait_ge(x1_T_made, WINDOWS)

            x1_T = even[:].rearrange("p w d -> p (w d)")

            def mlp(b, windows):
                n = windows * P
                for j in range(HJ):
                    after(pe, gelu_made, b * HJ + j - 1)
                    for c in range(CH):
                        if windows == 1:
                            rhs = x1_T[:, b * BLOCK * DIM + c * P:b * BLOCK * DIM + (c + 1) * P]
                        else:
                            rhs = x1_T[:, bass.ds(b * (BLOCK * DIM), BLOCK * DIM)].rearrange(
                                "p (v d) -> p v d", v=BLOCK)[:, :, c * P:(c + 1) * P]
                        last = nc.tensor.matmul(mlp1_ps[:, j % 2, 0:n], w1_sb[:, c, j * P:(j + 1) * P], rhs,
                                                start=(c == 0), stop=(c == CH - 1))
                    last.then_inc(mlp1_summed, 1)
                pe.wait_ge(gelu_made, b * HJ + HJ)
                for v in range(windows):
                    after(pe, biased_made, b * BLOCK + v - 1)
                    for j in range(HJ):
                        last = nc.tensor.matmul(mlp2_ps[:, v % 2, 0:DIM], hidden2_T[:, j, v * P:(v + 1) * P],
                                                w2_sb[:, j, :], start=(j == 0), stop=(j == HJ - 1))
                    last.then_inc(mlp2_summed, 1)

            rolled(pe, BLOCKS, lambda b: mlp(b, BLOCK), 1)
            mlp(BLOCKS, 1)


def kernel(x, src, dst, edge_attr_64, L0_gnn_W_x, L0_gnn_W_e, L0_gnn_att_a, L0_gnn_W_ff1, L0_gnn_W_ff2,
           L0_ffn_attention_mask, L0_ffn_wr, L0_ffn_br, L0_ffn_w1, L0_ffn_b1, L0_ffn_w2, L0_ffn_b2):
    import numpy as np
    import concourse.bacc as bacc
    from concourse.bass_utils import run_bass_kernel_spmd

    def padded(a, fill):
        a = np.asarray(a)
        return np.concatenate([a, np.full((EP - E,) + a.shape[1:], fill, a.dtype)])

    src_p, dst_p = padded(src, 0), padded(dst, NP - 1)
    edges = padded(edge_attr_64, 0).reshape(GROUPS, 2, 2, P, EDGE_DIM).transpose(1, 4, 0, 2, 3)
    arrays = {
        "x": x, "src": src_p.reshape(TILES, P).T, "dst": dst_p.reshape(TILES, P).T,
        "group_last": dst_p[GROUP - 1::GROUP].reshape(1, GROUPS),
        "edges": edges.reshape(2 * EDGE_DIM, GROUPS * 2 * P),
        "W_x": L0_gnn_W_x, "W_e": L0_gnn_W_e, "att": np.asarray(L0_gnn_att_a).reshape(1, DIM),
        "W_ff1": L0_gnn_W_ff1, "W_ff2": L0_gnn_W_ff2, "wr": np.asarray(L0_ffn_wr).reshape(1, DIM),
        "br": np.asarray(L0_ffn_br).reshape(1, 1), "w1": L0_ffn_w1, "b1": L0_ffn_b1, "w2": L0_ffn_w2,
        "b2": np.asarray(L0_ffn_b2).reshape(1, DIM),
    }
    arrays = {name: np.ascontiguousarray(a) for name, a in arrays.items()}
    nc = bacc.Bacc("TRN2", target_bir_lowering=False, num_devices=1)
    args = [nc.dram_tensor(name, a.shape, mybir.dt.from_np(a.dtype), kind="ExternalInput").ap()
            for name, a in arrays.items()]
    out = nc.dram_tensor("out", (N, DIM), F32, kind="ExternalOutput").ap()
    build(nc, *args, out)
    return run_bass_kernel_spmd(nc, [arrays], core_ids=[0]).results[0]["out"]
```

```python
from contextlib import ExitStack

import concourse.bass as bass
from concourse import mybir

P = 128
DIM = 256
CH = DIM // P
EDGE_DIM = 64
HEADS = 4
HEAD_DIM = DIM // HEADS
HOPS = 3
GAMMA = 0.5
FF = 512
FFJ = FF // P
HID = 1024
HJ = HID // P
EPS = 1e-5
N = 6250
WINDOWS = -(-N // P)
NP = WINDOWS * P
TAIL = N - (WINDOWS - 1) * P
E = 106250
TILES_IN_GROUP = 4
GROUP = TILES_IN_GROUP * P
RING = 4
TWO_RINGS = 2 * RING
UNROLL = 2 * TWO_RINGS
GROUPS = -(-E // (GROUP * UNROLL)) * UNROLL
TILES = GROUPS * TILES_IN_GROUP
EP = TILES * P
PREPARED = (WINDOWS - 1) // (GROUPS // UNROLL - 1)
assert 0 < WINDOWS - PREPARED * (GROUPS // UNROLL - 1)
VISITS = GROUPS + WINDOWS - 1
SELECTED = N // 2 - 1
WCOL = DIM + 1
SEVEN = 7
assert WINDOWS % SEVEN == 0
BLOCK = 4
BLOCKS = WINDOWS // BLOCK
LOWEST = -3.0e38
LAG = 5
EARLY = 4
STEPS = WINDOWS + LAG
assert STEPS % 2 == 0
TRIES = 4
SEARCH_BLOCKS = 8
assert TRIES * SEARCH_BLOCKS >= 31 and SEARCH_BLOCKS + 1 < BLOCKS

ALU = mybir.AluOpType
ACT = mybir.ActivationFunctionType
AX = mybir.AxisListType.X
F32 = mybir.dt.float32
I32 = mybir.dt.int32


def build(nc, x, src, dst, group_last, edges, W_x, W_e, att, W_ff1, W_ff2, wr, br, w1, b1, w2, b2, out):
    with ExitStack() as ctx:
        def sb(name, shape, dt=F32):
            return ctx.enter_context(nc.sbuf_tensor(name, shape, dt))

        def sem(name):
            return ctx.enter_context(nc.semaphore(name))

        tables = [nc.dram_tensor(f"hop_table{k}", (NP, DIM), F32, kind="Internal").ap() for k in range(HOPS)]

        even = sb("even", [P, WINDOWS, DIM])
        odd = sb("odd", [P, WINDOWS, WCOL])
        neighbours = sb("neighbours", [P, RING, TILES_IN_GROUP, DIM])
        edge_ring = sb("edge_ring", [P, RING, 2, P])
        sums = sb("sums", [P, 2, TILES_IN_GROUP, DIM])
        messages = sb("messages", [P, 2, TILES_IN_GROUP, WCOL])
        onehot = sb("onehot", [P, 3, TILES_IN_GROUP, P])
        src_all = sb("src_all", [P, TILES], I32)
        src_now = sb("src_now", [P, 2, RING * TILES_IN_GROUP], I32)
        dst_int = sb("dst_int", [P, TILES], I32)
        dst_all = sb("dst_all", [P, TILES])
        last_dst = sb("last_dst", [1, GROUPS], I32)
        first_window = sb("first_window", [1, GROUPS + 1], I32)
        node_row = sb("node_row", [P, P])
        window_base = sb("window_base", [P, WINDOWS])
        ident = sb("ident", [P, P])
        ones = sb("ones", [P, P])
        below = sb("below", [P, P])
        wx_sb = sb("wx_sb", [P, CH, DIM])
        we_sb = sb("we_sb", [P, DIM])
        wff1_sb = sb("wff1_sb", [P, CH, FF])
        wff2_sb = sb("wff2_sb", [P, FFJ, DIM])
        w1_sb = sb("w1_sb", [P, CH, HID])
        w2_sb = sb("w2_sb", [P, HJ, DIM])
        b1_sb = sb("b1_sb", [P, HJ])
        rows = sb("rows", [1, 3 * DIM + 1])
        rows_all = sb("rows_all", [P, 3 * DIM + 1])
        att_all = rows_all[:, 0:DIM]
        wr_all = rows_all[:, DIM:2 * DIM]
        b2_all = rows_all[:, 2 * DIM:3 * DIM]
        br_all = rows_all[:, 3 * DIM:3 * DIM + 1]
        half_degree = sb("half_degree", [P, WINDOWS])
        stats = sb("stats", [P, 6 * SEVEN])
        aggregates = sb("aggregates", [P, 2 * SEVEN])
        roots_plus = sb("roots_plus", [P, WINDOWS])
        minus_means = sb("minus_means", [P, WINDOWS])
        moment = sb("moment", [P, 2 * WINDOWS])
        roots = sb("roots", [P, WINDOWS])
        root_t = sb("root_t", [P, WINDOWS])
        root_v = sb("root_v", [P, WINDOWS])
        ring_flat = neighbours[:].rearrange("p r t d -> p (r t d)")
        sums_flat = sums[:].rearrange("p r t d -> p (r t d)")
        normal = [ring_flat[:, b * DIM:(b + 1) * DIM] for b in range(2 * SEVEN)]
        normal_T = [ring_flat[:, (2 * SEVEN + b) * DIM:(2 * SEVEN + 1 + b) * DIM] for b in range(2)]

        e_ps = ctx.enter_context(nc.psum_tensor("e_ps", [P, 2, TILES_IN_GROUP * DIM], F32))
        sum_ps = ctx.enter_context(nc.psum_tensor("sum_ps", [P, 2, 512], F32))
        more_ps = ctx.enter_context(nc.psum_tensor("more_ps", [P, 2, 512], F32))
        visit_ps = [sum_ps[:, 0], sum_ps[:, 1], more_ps[:, 0]]
        EXTRA = 2

        x_landed = [sem(f"x_landed{part}") for part in range(SEVEN)]
        tables_landed = sem("tables_landed")
        node_weights_landed = sem("node_weights_landed")
        weights_landed = sem("weights_landed")
        rows_landed = sem("rows_landed")
        consts_made = sem("consts_made")
        CONSTS = 10
        rows_made = sem("rows_made")
        dve_step = sem("dve_step")
        normal_made = sem("normal_made")
        normal_turned = sem("normal_turned")
        normal_T_made = sem("normal_T_made")
        h0_summed = sem("h0_summed")
        h0_made = sem("h0_made")
        cleared = sem("cleared")
        published = sem("published")
        edge_landed = [sem(f"edge_landed{r}") for r in range(RING)]
        gathered = [sem(f"gathered{r}") for r in range(RING)]
        src_staged = sem("src_staged")
        edge_multiplied = sem("edge_multiplied")
        added = sem("added")
        relued = sem("relued")
        onehot_ready = sem("onehot_ready")
        extra_ready = sem("extra_ready")
        scattered = sem("scattered")
        flushed = sem("flushed")
        window_done = sem("window_done")
        hop_started = sem("hop_started")

        block = ctx.enter_context(nc.Block())

        def rolled(eng, n, body, head):
            for i in range(head):
                body(i)
            with eng.Fori(head, n) as i:
                body(i)

        def stage(fn, w, p):
            if not isinstance(w, int) or 0 <= w < WINDOWS:
                fn(w, p)

        def after(eng, s, count):
            if not (isinstance(count, int) and count <= 0):
                eng.wait_ge(s, count)

        def next_window(w):
            return (w + 1).with_bounds(min_val=1, max_val=WINDOWS - 1)

        def load_windows(eng, it):
            return nc.values_load_multi_w_load_instructions(
                first_window[:, bass.ds(it * UNROLL, UNROLL + 1)], engines=(eng.engine,), min_val=0,
                max_val=WINDOWS - 1)[1]

        def window(ap, w, width, n):
            return ap[:, bass.ds(w * width, n)]

        even_flat = even[:].rearrange("p w d -> p (w d)")
        odd_flat = odd[:].rearrange("p w d -> p (w d)")

        def state(k, w, n=DIM):
            return window(even_flat, w, DIM, n) if k % 2 == 0 else window(odd_flat, w, WCOL, n)

        def early(w, k, first=0, n=DIM):
            return early_flat[:, bass.ds(w % EARLY * (2 * DIM) + (k * DIM + first), n)]

        def past(w, k):
            return past_flat[:, bass.ds(w % 2 * (2 * DIM) + k * DIM, DIM)]

        def x_row(w):
            return x_flat[:, bass.ds(w % 2 * DIM, DIM)]

        def product(i):
            return (sums_flat, messages_flat)[i % 2][:, 0:SEVEN * DIM].rearrange("p (w d) -> p w d", d=DIM)

        def in_two_parts(eng, steps):
            steps(0, 2 * SEVEN)
            with eng.Fori(1, WINDOWS // (2 * SEVEN)) as i:
                steps(i * (2 * SEVEN), 2 * SEVEN)
            steps(WINDOWS - SEVEN, SEVEN)

        def in_pairs(eng, step):
            for i in range(LAG + 1):
                step(i, i % 2)
            with eng.Fori((LAG + 1) // 2, (WINDOWS - 1) // 2) as pair:
                step(pair * 2, 0)
                step(pair * 2 + 1, 1)
            for i in range(WINDOWS - 1, STEPS):
                step(i, i % 2)

        def dram_rows(t, w):
            return t[bass.ds(w * P, P), :]

        turned_ps = [e_ps[:, 0, b * 512:b * 512 + DIM] for b in range(2)]
        h0_ps = [e_ps[:, 1, b * 512:b * 512 + DIM] for b in range(2)]

        early_flat = ring_flat[:, 0:EARLY * 2 * DIM]
        x_flat = ring_flat[:, 8 * DIM:10 * DIM]
        query = [ring_flat[:, b * DIM:(b + 1) * DIM] for b in (10, 12)]
        xln = ring_flat[:, 13 * DIM:14 * DIM]
        attended = [ring_flat[:, (14 + b) * DIM:(15 + b) * DIM] for b in range(2)]
        tanhs = sums_flat[:, 0:DIM]
        scaled = sums_flat[:, 4 * DIM:8 * DIM]
        weighed = ring_flat[:, 11 * DIM:12 * DIM]
        messages_flat = messages[:].rearrange("p r t d -> p (r t d)")
        hidden_T = messages_flat[:, 0:FF]
        ffsum = messages_flat[:, FF:FF + DIM]
        halves = messages_flat[:, FF + DIM:FF + 3 * DIM]
        attended_T = messages_flat[:, FF + 3 * DIM:FF + 4 * DIM]
        x1_block = onehot[:].rearrange("p s t d -> p (s t d)")[:, 0:BLOCK * DIM]
        past_flat = sb("past_flat", [P, 2 * 2 * DIM])
        past_query = sb("past_query", [P, 2 * DIM])
        past_tanhs = sb("past_tanhs", [P, 3 * DIM])
        past_weighed = sb("past_weighed", [P, 3 * DIM])
        scores = sb("scores", [P, WINDOWS * 4 * HEADS])
        maxs = sb("maxs", [P, HEADS])
        less = sb("less", [P, 4 * HEADS])
        exps = sb("exps", [P, 4 * HEADS])
        denominator = sb("denominator", [P, 2 * HEADS])
        alpha = sb("alpha", [P, 4 * HEADS])
        mlp_weight = sb("mlp_weight", [P, WINDOWS])
        attended_T_ps = e_ps[:, 0, 0:DIM]
        hidden_ps = e_ps[:, 0, 512:1024]
        ffsum_ps = e_ps[:, 1, 0:DIM]
        x1_T_ps = e_ps[:, 0, 0:BLOCK * DIM]
        total_ps = e_ps[:, 1, 0:1]
        equals_ps = e_ps[:, 1, 512:512 + 2 * WINDOWS]

        past_landed = sem("past_landed")
        past_queries_made = sem("past_queries_made")
        past_tanhs_made = sem("past_tanhs_made")
        past_weighed_made = sem("past_weighed_made")
        past_scored = sem("past_scored")
        early_landed = sem("early_landed")
        x_row_landed = sem("x_row_landed")
        xln_made = sem("xln_made")
        x1_rows_made = sem("x1_rows_made")
        products_made = sem("products_made")
        roots_made = sem("roots_made")
        router_made = sem("router_made")
        x1_plus_made = sem("x1_plus_made")
        x1_staged = sem("x1_staged")
        queries_made = sem("queries_made")
        tanhs_made = sem("tanhs_made")
        less_made = sem("less_made")
        exps_made = sem("exps_made")
        alpha_made = sem("alpha_made")
        scaled_made = sem("scaled_made")
        attended_made = sem("attended_made")
        attended_turned = sem("attended_turned")
        attended_T_made = sem("attended_T_made")
        hidden_summed = sem("hidden_summed")
        hidden_made = sem("hidden_made")
        ff_summed = sem("ff_summed")
        x1_made = sem("x1_made")
        x1_ln_made = sem("x1_ln_made")
        x1_turned = sem("x1_turned")
        x1_T_made = sem("x1_T_made")
        search = sb("search", [P, 16])
        found = sb("found", [P, WINDOWS])
        equals = sb("equals", [P, WINDOWS])
        prefix = sb("prefix", [P, WINDOWS])
        chosen = sb("chosen", [P, WINDOWS])
        counts_made = sem("counts_made")
        totals_made = sem("totals_made")
        chosen_made = sem("chosen_made")
        hidden2_T = ring_flat[:, 0:HJ * BLOCK * P].rearrange("p (j n) -> p j n", j=HJ)
        mlp1_summed = sem("mlp1_summed")
        gelu_made = sem("gelu_made")
        biased_made = sem("biased_made")
        window_table_made = sem("window_table_made")
        mlp2_summed = sem("mlp2_summed")
        result_made = sem("result_made")
        out_stored = sem("out_stored")
        mlp1_ps = more_ps
        mlp2_ps = sum_ps

        @block.sync
        def _(sp):
            for part in range(SEVEN - 1):
                first = part * (WINDOWS // SEVEN)
                last = first + WINDOWS // SEVEN
                sp.dma_start(odd[:, first:last, 0:DIM],
                             x[first * P:last * P, :].rearrange("(w p) d -> p w d", p=P)).then_inc(x_landed[part], 16)
            sp.dma_start(odd[:, last:WINDOWS - 1, 0:DIM],
                         x[last * P:(WINDOWS - 1) * P, :].rearrange("(w p) d -> p w d", p=P)
                         ).then_inc(x_landed[SEVEN - 1], 16)
            sp.wait_ge(consts_made, 1)
            sp.dma_start(odd[0:TAIL, WINDOWS - 1, 0:DIM], x[(WINDOWS - 1) * P:N, :]).then_inc(x_landed[SEVEN - 1], 16)
            sp.dma_start(wff1_sb[:], W_ff1.rearrange("(c p) n -> p c n", p=P)).then_inc(weights_landed, 16)
            sp.dma_start(wff2_sb[:], W_ff2.rearrange("(c p) n -> p c n", p=P)).then_inc(weights_landed, 16)
            sp.dma_start(w1_sb[:], w1.rearrange("(c p) n -> p c n", p=P)).then_inc(weights_landed, 16)
            sp.dma_start(w2_sb[:], w2.rearrange("(c p) n -> p c n", p=P)).then_inc(weights_landed, 16)
            with nc.allow_non_contiguous_dma(reason="1024 numbers, once"):
                sp.dma_start(b1_sb[:], b1.rearrange("(j p) -> p j", p=P)).then_inc(weights_landed, 16)
            sp.dma_start(rows[:, 0:DIM], att).then_inc(rows_landed, 16)
            sp.dma_start(rows[:, DIM:2 * DIM], wr).then_inc(rows_landed, 16)
            sp.dma_start(rows[:, 2 * DIM:3 * DIM], b2).then_inc(rows_landed, 16)
            sp.dma_start(rows[:, 3 * DIM:3 * DIM + 1], br).then_inc(rows_landed, 16)

            with sp.Fori(0, WINDOWS) as w:
                sp.wait_ge(h0_made, w + 1)
                sp.dma_start(dram_rows(tables[0], w), state(0, w)).then_inc(published, 16)

            for k in range(HOPS - 1):
                with sp.Fori(0, WINDOWS) as w:
                    sp.wait_ge(window_done, w + (k * WINDOWS + 1))
                    sp.dma_start(dram_rows(tables[k + 1], w), state(k + 1, w)).then_inc(published, 16)

            def load_past(w):
                after(sp, past_tanhs_made, w - 1)
                sp.nop(nofuse=True)
                after(sp, past_landed, w * 32)
                sp.nop(nofuse=True)
                for k in range(2):
                    sp.dma_start(past(w, k), dram_rows(tables[k], w)).then_inc(past_landed, 16)

            sp.wait_ge(published, 16 * WINDOWS * HOPS)
            rolled(sp, WINDOWS, load_past, 2)

            sp.wait_ge(published, 16 * WINDOWS * HOPS)
            sp.wait_ge(added, RING + HOPS * GROUPS)

            def load_early(w, p):
                after(sp, scaled_made, w - EARLY + 1)
                sp.nop(nofuse=True)
                after(sp, early_landed, w * 32)
                sp.nop(nofuse=True)
                for k in range(2):
                    sp.dma_start(early(w, k), dram_rows(tables[k], w)).then_inc(early_landed, 16)

            def load_x(w, p):
                after(sp, xln_made, w - 1)
                sp.nop(nofuse=True)
                after(sp, x_row_landed, w * 16)
                sp.nop(nofuse=True)
                if isinstance(w, int) and w == WINDOWS - 1:
                    sp.dma_start(x_row(w)[0:TAIL, :], x[w * P:N, :]).then_inc(x_row_landed, 16)
                else:
                    sp.dma_start(x_row(w), dram_rows(x, w)).then_inc(x_row_landed, 16)

            def load_step(i, p):
                stage(load_early, i, p)
                stage(load_x, i - 3, 1 - p)

            in_pairs(sp, load_step)

            with sp.Fori(0, BLOCKS) as b:
                sp.wait_ge(result_made, b * BLOCK + BLOCK)
                sp.dma_start(out[bass.ds(b * (BLOCK * P), BLOCK * P), :].rearrange("(v p) d -> p v d", p=P),
                             odd_flat[:, bass.ds(b * (BLOCK * WCOL), BLOCK * WCOL)].rearrange(
                                 "p (v d) -> p v d", v=BLOCK)[:, :, 0:DIM]).then_inc(out_stored, 16)
            sp.wait_ge(result_made, WINDOWS)
            sp.dma_start(out[(WINDOWS - 1) * P:N, :], odd[0:TAIL, WINDOWS - 1, 0:DIM]).then_inc(out_stored, 16)
            sp.wait_ge(out_stored, 16 * (BLOCKS + 1))

        @block.gpsimd
        def _(pool):
            nc.gpsimd.memset(odd[:, WINDOWS - 1, :], 0.0).then_inc(consts_made, 1)
            nc.gpsimd.memset(ident[:], 0.0).then_inc(consts_made, 1)
            nc.gpsimd.memset(below[:], 1.0).then_inc(consts_made, 1)
            pool.wait_ge(consts_made, 3)
            nc.gpsimd.affine_select(out=ident[:], in_=ident[:], compare_op=ALU.not_equal, fill=1.0, base=0,
                                    pattern=[[-1, P]], channel_multiplier=1).then_inc(consts_made, 1)
            nc.gpsimd.affine_select(out=below[:], in_=below[:], compare_op=ALU.is_gt, fill=0.0, base=0,
                                    pattern=[[1, P]], channel_multiplier=-1).then_inc(consts_made, 1)
            nc.gpsimd.iota(node_row[:], pattern=[[1, P]], base=0, channel_multiplier=0,
                           allow_small_or_imprecise_dtypes=True).then_inc(consts_made, 1)
            nc.gpsimd.iota(window_base[:], pattern=[[P, WINDOWS]], base=0, channel_multiplier=0,
                           allow_small_or_imprecise_dtypes=True).then_inc(consts_made, 1)
            nc.gpsimd.memset(messages[:], 1.0).then_inc(consts_made, 1)
            nc.gpsimd.memset(first_window[:, 0:1], 0).then_inc(consts_made, 1)
            nc.gpsimd.memset(ones[:], 1.0).then_inc(consts_made, 1)
            for part in range(SEVEN):
                pool.wait_ge(normal_made, (part + 1) * SEVEN)
                nc.gpsimd.memset(odd[:, part * SEVEN:(part + 1) * SEVEN, :], 0.0).then_inc(cleared, 1)
            pool.wait_ge(rows_landed, 64)
            nc.gpsimd.partition_broadcast(rows_all[:], rows[:], channels=P).then_inc(rows_made, 1)
            pool.wait_ge(tables_landed, 48)
            for k in range(HOPS):
                pool.wait_ge(published, 16 * WINDOWS * (k + 1))
                if k == 0:
                    pool.wait_ge(h0_summed, WINDOWS)
                with pool.Fori(0, GROUPS // TWO_RINGS) as it:
                    for u in range(TWO_RINGS):
                        r = u % RING
                        g = it * TWO_RINGS + u + k * GROUPS
                        half = u // RING
                        pool.wait_ge(added, g + 1)
                        if r == 0:
                            pool.nop(nofuse=True)
                            cols = bass.ds(it * (TWO_RINGS * TILES_IN_GROUP) + half * RING * TILES_IN_GROUP,
                                           RING * TILES_IN_GROUP)
                            nc.gpsimd.tensor_copy(src_now[:, half, :], src_all[:, cols]).then_inc(src_staged, 1)
                            pool.wait_ge(src_staged, it * 2 + (half + 1 + 2 * k * (GROUPS // TWO_RINGS)))
                        pool.nop(nofuse=True)
                        for t in range(TILES_IN_GROUP):
                            i = r * TILES_IN_GROUP + t
                            nc.gpsimd.indirect_dma_start(
                                out=neighbours[:, r, t, :], out_offset=None, in_=tables[k],
                                in_offset=bass.IndirectOffsetOnAxis(ap=src_now[:, half, i:i + 1], axis=0),
                            ).then_inc(gathered[r], 16)

            def query_stage(w, p):
                pool.wait_ge(early_landed, w * 32 + 32)
                after(pool, tanhs_made, w - 1)
                pool.nop(nofuse=True)
                nc.gpsimd.tensor_tensor(query[p], state(3, w), early(w, 0), ALU.add).then_inc(queries_made, 1)

            def scale_stage(w, p):
                pool.wait_ge(alpha_made, w + 1)
                after(pool, attended_made, w)
                pool.nop(nofuse=True)
                for k in range(HOPS + 1):
                    h = early(w, k) if k < 2 else state(k, w)
                    last = nc.gpsimd.tensor_tensor(
                        scaled[:, k * DIM:(k + 1) * DIM].rearrange("p (h d) -> p h d", h=HEADS),
                        h.rearrange("p (h d) -> p h d", h=HEADS),
                        alpha[:, k * HEADS:(k + 1) * HEADS].unsqueeze(2).broadcast_to([P, HEADS, HEAD_DIM]), ALU.mult)
                last.then_inc(scaled_made, 1)

            def attend_step(i, p):
                stage(query_stage, i, p)
                stage(scale_stage, i - 2, p)

            pool.wait_ge(window_done, WINDOWS * HOPS)
            in_pairs(pool, attend_step)

            def multiply_route(i):
                pool.wait_ge(x1_ln_made, i * SEVEN + SEVEN)
                after(pool, router_made, i - 1)
                nc.gpsimd.tensor_tensor(
                    product(i), even[:, i * SEVEN:(i + 1) * SEVEN, :],
                    wr_all.unsqueeze(1).broadcast_to([P, SEVEN, DIM]), ALU.mult).then_inc(products_made, 1)

            def stage_block(b, windows):
                after(pool, x1_turned, b)
                pool.nop(nofuse=True)
                nc.gpsimd.tensor_copy(x1_block[:, 0:windows * DIM],
                                      even_flat[:, bass.ds(b * (BLOCK * DIM), windows * DIM)]).then_inc(x1_staged, 1)

            pool.wait_ge(roots_made, 1)
            for i in range(WINDOWS // SEVEN):
                multiply_route(i)
                if i < 2:
                    stage_block(i, BLOCK)
            with pool.Fori(2, BLOCKS) as b:
                stage_block(b, BLOCK)
            stage_block(BLOCKS, 1)

        @block.scalar
        def _(act):
            act.dma_start(wx_sb[:], W_x.rearrange("(c p) n -> p c n", p=P)).then_inc(node_weights_landed, 16)
            for h in range(2):
                act.dma_start(we_sb[h * EDGE_DIM:(h + 1) * EDGE_DIM, :], W_e).then_inc(node_weights_landed, 16)
            act.dma_start(src_all[:], src).then_inc(tables_landed, 16)
            act.dma_start(dst_int[:], dst).then_inc(tables_landed, 16)
            act.dma_start(last_dst[:], group_last).then_inc(tables_landed, 16)

            def copy_turned_rows(w, u):
                act.wait_ge(normal_turned, w + 1)
                after(act, h0_summed, w - 1)
                nc.scalar.copy(normal_T[u % 2], turned_ps[u % 2]).then_inc(normal_T_made, 1)

            def copy_h0(w, u):
                act.wait_ge(h0_summed, w + 1)
                act.nop(nofuse=True)
                nc.scalar.copy(state(0, w), h0_ps[u % 2]).then_inc(h0_made, 1)

            def node_steps(first, n):
                for u in range(n):
                    copy_turned_rows(first + u, u)
                    if u:
                        copy_h0(first + u - 1, u - 1)
                copy_h0(first + n - 1, n - 1)

            in_two_parts(act, node_steps)

            def load_edges(k, g, u):
                act.wait_ge(edge_multiplied, g + (k * GROUPS + 1))
                act.dma_start(edge_ring[:, u % RING],
                              edges[:, bass.ds(g * 2 * P, 2 * P)].rearrange("p (j e) -> p j e", j=2)
                              ).then_inc(edge_landed[u % RING], 16)

            act.sem_inc(relued, 2)
            for k in range(HOPS):
                load_edges(k, 0, 0)
                load_edges(k, 1, 1)

                def past_tanh(w):
                    act.wait_ge(past_landed, w * 32 + 32)
                    act.wait_ge(past_queries_made, w + 1)
                    after(act, past_weighed_made, w)
                    act.nop(nofuse=True)
                    nc.scalar.activation(past_tanhs[:, 0:DIM], past(w, 0), ACT.Tanh, scale=2.0)
                    nc.scalar.activation(past_tanhs[:, DIM:3 * DIM], past_query[:],
                                         ACT.Tanh).then_inc(past_tanhs_made, 1)

                def rectify(it, last, past_window=None):
                    for u in range(RING):
                        g = it * RING + u
                        if not last or u + 2 < RING:
                            load_edges(k, g + 2, u + 2)
                        act.wait_ge(added, g + (RING + k * GROUPS + 1))
                        if k == 0 and u < 2:
                            act.wait_ge(consts_made, CONSTS)
                        nc.scalar.activation(messages[:, u % 2, :, 0:DIM], sums[:, u % 2], ACT.Relu).then_inc(relued, 1)
                        if past_window is not None and u == 1:
                            past_tanh(past_window)

                tanh_steps = WINDOWS if k == HOPS - 1 else 0
                if tanh_steps:
                    rectify(0, False, 0)
                    with act.Fori(1, tanh_steps) as it:
                        rectify(it, False, it)
                with act.Fori(tanh_steps, GROUPS // RING - 1) as it:
                    rectify(it, False)
                rectify(GROUPS // RING - 1, True)

            def tanh_stage(w, p):
                act.wait_ge(queries_made, w + 1)
                after(act, less_made, w)
                nc.scalar.activation(tanhs, query[p], ACT.Tanh).then_inc(tanhs_made, 1)

            def turned_stage(w, p):
                act.wait_ge(attended_turned, w + 1)
                nc.scalar.copy(attended_T, attended_T_ps).then_inc(attended_T_made, 1)

            def xln_stage(w, p):
                act.wait_ge(x_row_landed, w * 16 + 16)
                after(act, x1_made, w)
                act.nop(nofuse=True)
                nc.scalar.activation(xln, x_row(w), ACT.Identity, scale=roots_plus[:, bass.ds(w, 1)],
                                     bias=minus_means[:, bass.ds(w, 1)]).then_inc(xln_made, 1)

            def exp_stage(w, p):
                act.wait_ge(less_made, w + 1)
                after(act, alpha_made, w)
                nc.scalar.activation(exps[:], less[:], ACT.Exp).then_inc(exps_made, 1)

            def hidden_stage(w, p):
                act.wait_ge(hidden_summed, w + 1)
                nc.scalar.activation(hidden_T, hidden_ps, ACT.Relu).then_inc(hidden_made, 1)

            def attend_step(i, p):
                stage(tanh_stage, i, p)
                stage(turned_stage, i - 2, p)
                stage(xln_stage, i - 3, 1 - p)
                stage(exp_stage, i, p)
                stage(hidden_stage, i - 2, p)

            act.wait_ge(window_done, WINDOWS * HOPS)
            in_pairs(act, attend_step)

            def copy_turned(b, windows):
                act.wait_ge(x1_turned, b + 1)
                act.nop(nofuse=True)
                nc.scalar.copy(even_flat[:, bass.ds(b * (BLOCK * DIM), windows * DIM)],
                               x1_T_ps[:, 0:windows * DIM]).then_inc(x1_T_made, 1)

            def gelus(b, width):
                for j in range(HJ):
                    act.wait_ge(mlp1_summed, b * HJ + j + 1)
                    if j == 0:
                        after(act, mlp2_summed, b * BLOCK)
                    nc.scalar.activation(hidden2_T[:, j, 0:width], mlp1_ps[:, j % 2, 0:width], ACT.Gelu_apprx_tanh,
                                         bias=b1_sb[:, j:j + 1]).then_inc(gelu_made, 1)

            def add_residual(b, windows):
                for v in range(windows):
                    w = b * BLOCK + v
                    nc.scalar.activation(state(3, w), state(3, w), ACT.Identity, scale=roots_plus[:, bass.ds(w, 1)],
                                         bias=minus_means[:, bass.ds(w, 1)]).then_inc(x1_plus_made, 1)

            def mlp_block(b, more):
                gelus(b, BLOCK * P)
                copy_turned(b + 1, more)
                add_residual(b, BLOCK)

            act.wait_ge(roots_made, 1)
            act.wait_ge(products_made, 1)
            copy_turned(0, BLOCK)
            gelus(0, BLOCK * P)
            act.wait_ge(x1_ln_made, WINDOWS)
            act.wait_ge(products_made, 2)
            copy_turned(1, BLOCK)
            add_residual(0, BLOCK)
            act.wait_ge(products_made, SEVEN)
            with act.Fori(1, BLOCKS - 1) as b:
                mlp_block(b, BLOCK)
            mlp_block(BLOCKS - 1, 1)
            gelus(BLOCKS, P)
            add_residual(BLOCKS, 1)

        @block.vector
        def _(dve):
            chain = [0, 0]

            def link(ins):
                ins.then_inc(dve_step, 1)
                chain[1] += 1
                dve.wait_ge(dve_step, chain[0] + chain[1])

            def step(ins):
                ins.then_inc(dve_step, 1)
                chain[1] += 1
                return chain[1]

            def need(n):
                dve.wait_ge(dve_step, chain[0] + n)

            def rolled_links(n, body, head):
                for i in range(head):
                    before = chain[1]
                    body(i)
                each, before = chain[1] - before, chain[1]
                with dve.Fori(head, n) as i:
                    chain[:] = [(i - head) * each, before]
                    body(i)
                chain[:] = [0, before + each * (n - head)]

            def in_pairs_links(step):
                for i in range(LAG + 1):
                    before = chain[1]
                    step(i, i % 2)
                first, end = (LAG + 1) // 2, (WINDOWS - 1) // 2
                each, before = 2 * (chain[1] - before), chain[1]
                with dve.Fori(first, end) as pair:
                    chain[:] = [(pair - first) * each, before]
                    step(pair * 2, 0)
                    step(pair * 2 + 1, 1)
                chain[:] = [0, before + each * (end - first)]
                for i in range(WINDOWS - 1, STEPS):
                    step(i, i % 2)

            dve.sem_inc(added, RING)
            dve.sem_inc(flushed, 1)
            def rsqrt(root, value, t, v):
                link(nc.vector.tensor_scalar(v, value, EPS, None, ALU.add))
                link(nc.vector.tensor_single_scalar(t.bitcast(I32), v.bitcast(I32), 1, op=ALU.logical_shift_right))
                link(nc.vector.tensor_scalar(root.bitcast(I32), t.bitcast(I32), -1.0, float(0x5F3759DF),
                                             ALU.mult, ALU.add))
                link(nc.vector.tensor_tensor(t, root, root, ALU.mult))
                for i in range(3):
                    link(nc.vector.tensor_tensor(t, t, v, ALU.mult))
                    link(nc.vector.tensor_scalar(t, t, -0.5, 1.5, ALU.mult, ALU.add))
                    link(nc.vector.tensor_tensor(root, root, t, ALU.mult))
                    if i < 2:
                        link(nc.vector.tensor_tensor(t, root, root, ALU.mult))

            def moments(i):
                for u in range(SEVEN):
                    ins = nc.vector.bn_stats(stats[:, u * 6:u * 6 + 6], state(1, i * SEVEN + u))
                link(ins)
                for u in range(SEVEN):
                    ins = nc.vector.bn_aggr(aggregates[:, 2 * u:2 * u + 2], stats[:, u * 6:u * 6 + 6])
                link(ins)
                link(nc.vector.tensor_copy(moment[:, i * 2 * SEVEN:(i + 1) * 2 * SEVEN], aggregates[:]))

            mean, variance = (moment[:].rearrange("p (w two) -> p w two", two=2)[:, :, c] for c in range(2))
            for part in range(SEVEN):
                dve.wait_ge(x_landed[part], 32 if part == SEVEN - 1 else 16)
                moments(part)
                cols = slice(part * SEVEN, (part + 1) * SEVEN)
                rsqrt(roots[:, cols], variance[:, cols], root_t[:, cols], root_v[:, cols])
                if part >= 2:
                    dve.wait_ge(normal_turned, (part - 1) * SEVEN)
                for w in range(part * SEVEN, (part + 1) * SEVEN):
                    nc.vector.tensor_scalar(normal[w % (2 * SEVEN)], state(1, w), moment[:, 2 * w:2 * w + 1],
                                            roots[:, w:w + 1], ALU.subtract, ALU.mult).then_inc(normal_made, 1)
            link(nc.vector.tensor_scalar(roots_plus[:], roots[:], 1.0, None, ALU.add))
            link(nc.vector.scalar_tensor_tensor(out=minus_means[:], in0=mean, scalar=-1.0, in1=roots[:],
                                                op0=ALU.mult, op1=ALU.mult))
            dve.wait_ge(tables_landed, 48)
            dve.wait_ge(consts_made, CONSTS)
            link(nc.vector.tensor_copy(dst_all[:], dst_int[:]))
            nc.vector.tensor_single_scalar(first_window[:, 1:GROUPS + 1], last_dst[:], P.bit_length() - 1,
                                           op=ALU.arith_shift_right).then_inc(window_table_made, 1)
            dve.wait_ge(window_table_made, 1)
            dve.wait_ge(cleared, SEVEN)

            for k in range(HOPS):
                if k == 1:
                    link(nc.vector.tensor_scalar(half_degree[:], odd[:, :, DIM:WCOL].rearrange("p w o -> p (w o)"),
                                                 -GAMMA, None, ALU.mult))
                    dve.wait_ge(published, 16 * WINDOWS)
                    link(nc.vector.tensor_tensor(even[:], even[:],
                                                 half_degree[:].unsqueeze(2).broadcast_to([P, WINDOWS, DIM]), ALU.mult))
                width = WCOL if k == 0 else DIM

                def add(it, u):
                    r = u % RING
                    use = it * (UNROLL // RING) + u // RING + k * (GROUPS // RING)
                    dve.wait_ge(edge_multiplied, it * UNROLL + (u + k * GROUPS + RING + 1))
                    dve.wait_ge(relued, it * UNROLL + (u + k * GROUPS + 1))
                    dve.wait_ge(gathered[r], (use + 1) * (16 * TILES_IN_GROUP))
                    nc.vector.tensor_tensor(sums[:, u % 2].rearrange("p t d -> p (t d)"), e_ps[:, u % 2, :],
                                            neighbours[:, r].rearrange("p t d -> p (t d)"), ALU.add).then_inc(added, 1)

                def make_onehot(it, u, w, slot):
                    d = dst_all[:, bass.ds(it * (UNROLL * TILES_IN_GROUP) + u * TILES_IN_GROUP, TILES_IN_GROUP)]
                    nc.vector.scalar_tensor_tensor(
                        out=onehot[:, slot],
                        in0=node_row[:].unsqueeze(1).broadcast_to([P, TILES_IN_GROUP, P]),
                        scalar=window_base[:, bass.ds(w, 1)],
                        in1=d.unsqueeze(2).broadcast_to([P, TILES_IN_GROUP, P]),
                        op0=ALU.add, op1=ALU.is_equal).then_inc(extra_ready if slot == EXTRA else onehot_ready, 1)

                def flush(it, u, w, slot):
                    visit = it * UNROLL + w + (u + k * VISITS)
                    dve.wait_ge(scattered, visit + 1)
                    dve.wait_ge(flushed, visit + 1)
                    acc = state(k + 1, w, width)
                    nc.vector.tensor_tensor(acc, visit_ps[slot][:, 0:width], acc, ALU.add).then_inc(flushed, 1)

                def leave(it, u, w):
                    dve.wait_ge(flushed, it * UNROLL + w + (u + k * VISITS + 1))
                    dve.nop(nofuse=True)
                    nc.vector.engine_nop().then_inc(window_done, 1)

                def past_queries(w):
                    dve.wait_ge(past_landed, w * 32 + 32)
                    after(dve, past_tanhs_made, w)
                    dve.nop(nofuse=True)
                    nc.vector.tensor_tensor(past_query[:, 0:DIM], past(w, 1), past(w, 0), ALU.add)
                    nc.vector.tensor_tensor(past_query[:, DIM:2 * DIM], state(2, w), past(w, 0),
                                            ALU.add).then_inc(past_queries_made, 1)

                def past_scores(w):
                    dve.wait_ge(past_tanhs_made, w + 1)
                    after(dve, past_scored, w)
                    nc.vector.tensor_tensor(past_weighed[:].rearrange("p (k d) -> p k d", d=DIM),
                                            past_tanhs[:].rearrange("p (k d) -> p k d", d=DIM),
                                            att_all.unsqueeze(1).broadcast_to([P, 3, DIM]),
                                            ALU.mult).then_inc(past_weighed_made, 1)
                    dve.wait_ge(past_weighed_made, w + 1)
                    dve.nop(nofuse=True)
                    nc.vector.tensor_reduce(scores[:, bass.ds(w * (4 * HEADS), 3 * HEADS)],
                                            past_weighed[:].rearrange("p (s d) -> p s d", d=HEAD_DIM), AX,
                                            ALU.add).then_inc(past_scored, 1)

                def past_step(it, u):
                    w = it * (UNROLL // RING) + u // RING
                    if k < HOPS - 1 or isinstance(w, int) and w >= WINDOWS:
                        return
                    if u % RING == 0:
                        past_queries(w)
                    if u % RING == RING - 1:
                        past_scores(w)

                def walk(it, last):
                    ws = load_windows(dve, it)
                    for u in range(UNROLL):
                        with dve.If(ws[u] < ws[u + 1]):
                            make_onehot(it, u, next_window(ws[u]), EXTRA)
                        if not last or u + 1 < UNROLL:
                            add(it, u + 1)
                            make_onehot(it, u + 1, ws[u + 1], (u + 1) % 2)
                        past_step(it, u)
                        flush(it, u, ws[u], u % 2)
                        with dve.If(ws[u] < ws[u + 1]):
                            leave(it, u, next_window(ws[u]))
                            flush(it, u, next_window(ws[u]), EXTRA)
                            with dve.If(ws[u] + 1 < ws[u + 1]):
                                with dve.Fori(ws[u] + 2, ws[u + 1] + 1) as w:
                                    leave(it, u, w)
                                    make_onehot(it, u, w, EXTRA)
                                    flush(it, u, w, EXTRA)

                def prepare(it, windows):
                    h1 = odd_flat[:, bass.ds(it * (PREPARED * WCOL), windows * WCOL)].rearrange(
                        "p (w d) -> p w d", d=WCOL)[:, :, 0:DIM]
                    part = half_degree[:, bass.ds(it * PREPARED, windows)]
                    nc.vector.tensor_tensor(h1, h1, part.unsqueeze(2).broadcast_to([P, windows, DIM]),
                                            ALU.mult).then_inc(hop_started, 1)

                if k == 1:
                    dve.wait_ge(published, 16 * WINDOWS * 2)
                if k == 2:
                    dve.wait_ge(rows_made, 1)
                    dve.wait_ge(hop_started, GROUPS // UNROLL)
                add(0, 0)
                make_onehot(0, 0, 0, 0)
                with dve.Fori(0, GROUPS // UNROLL - 1) as it:
                    if k == 1:
                        prepare(it, PREPARED)
                    walk(it, False)
                if k == 1:
                    prepare(GROUPS // UNROLL - 1, WINDOWS - PREPARED * (GROUPS // UNROLL - 1))
                walk(GROUPS // UNROLL - 1, True)
                dve.wait_ge(flushed, 1 + (k + 1) * VISITS)
                nc.vector.engine_nop().then_inc(window_done, 1)

            def attend_step(i, p):
                a, b, c = i - 1, i - 2, i - 4
                has_a, has_b, has_c = (not isinstance(w, int) or 0 <= w < WINDOWS for w in (a, b, c))
                if has_a:
                    score = scores[:, bass.ds(a * (4 * HEADS), 4 * HEADS)]
                    dve.wait_ge(tanhs_made, a + 1)
                    weigh = step(nc.vector.tensor_tensor(weighed, tanhs, att_all, ALU.mult))
                if has_a:
                    need(weigh)
                    dve.nop(nofuse=True)
                    sum_score = step(nc.vector.tensor_reduce(scores[:, bass.ds(a * (4 * HEADS) + 3 * HEADS, HEADS)],
                                                             weighed.rearrange("p (s d) -> p s d", d=HEAD_DIM),
                                                             AX, ALU.add))
                if has_a:
                    need(sum_score)
                    dve.nop(nofuse=True)
                    largest = step(nc.vector.tensor_reduce(maxs[:], score.rearrange("p (k h) -> p h k", h=HEADS),
                                                           AX, ALU.max))
                if has_c:
                    dve.wait_ge(ff_summed, c + 1)
                    sum_ff = step(nc.vector.tensor_tensor(ffsum, ffsum_ps, attended[p], ALU.add))
                if has_a:
                    need(largest)
                    dve.nop(nofuse=True)
                    nc.vector.tensor_tensor(less[:].rearrange("p (k h) -> p k h", h=HEADS),
                                            score.rearrange("p (k h) -> p k h", h=HEADS),
                                            maxs[:].unsqueeze(1).broadcast_to([P, 4, HEADS]),
                                            ALU.subtract).then_inc(less_made, 1)
                if has_c:
                    need(sum_ff)
                    dve.wait_ge(xln_made, c + 1)
                    dve.nop(nofuse=True)
                    nc.vector.scalar_tensor_tensor(out=state(3, c), in0=ffsum, scalar=0.0, in1=xln, op0=ALU.max,
                                                   op1=ALU.add).then_inc(x1_made, 1)
                if has_b:
                    dve.wait_ge(scaled_made, b + 1)
                    after(dve, attended_made, b)
                    halve = step(nc.vector.tensor_tensor(halves, scaled[:, 0:2 * DIM], scaled[:, 2 * DIM:4 * DIM],
                                                         ALU.add))
                if has_c:
                    dve.wait_ge(x1_made, c + 1)
                    dve.nop(nofuse=True)
                    statistics = step(nc.vector.bn_stats(stats[:, 0:6], state(3, c)))
                if has_b:
                    need(halve)
                    after(dve, attended_turned, b - 1)
                    after(dve, x1_made, b - 1)
                    nc.vector.tensor_tensor(attended[p], halves[:, 0:DIM], halves[:, DIM:2 * DIM],
                                            ALU.add).then_inc(attended_made, 1)
                if has_c:
                    need(statistics)
                    after(dve, x1_rows_made, c)
                    dve.nop(nofuse=True)
                    aggregate = step(nc.vector.bn_aggr(aggregates[:, 0:2], stats[:, 0:6]))
                if has_a:
                    dve.wait_ge(exps_made, a + 1)
                    after(dve, alpha_made, a)
                    link(nc.vector.tensor_reduce(denominator[:, 0:HEADS],
                                                 exps[:].rearrange("p (k h) -> p h k", h=HEADS), AX, ALU.add))
                if has_c:
                    need(aggregate)
                    nc.vector.tensor_scalar(moment[:, bass.ds(c * 2, 2)], aggregates[:, 0:2], 1.0, None,
                                            ALU.mult).then_inc(x1_rows_made, 1)
                if has_a:
                    link(nc.vector.reciprocal(denominator[:, HEADS:2 * HEADS], denominator[:, 0:HEADS]))
                    after(dve, scaled_made, a)
                    nc.vector.tensor_tensor(alpha[:].rearrange("p (k h) -> p k h", h=HEADS),
                                            exps[:].rearrange("p (k h) -> p k h", h=HEADS),
                                            denominator[:, HEADS:2 * HEADS].unsqueeze(1).broadcast_to([P, 4, HEADS]),
                                            ALU.mult).then_inc(alpha_made, 1)

            dve.wait_ge(past_scored, WINDOWS)
            in_pairs_links(attend_step)
            dve.wait_ge(x1_rows_made, WINDOWS)
            dve.wait_ge(xln_made, WINDOWS)
            rsqrt(roots[:], variance, root_t[:], root_v[:])
            link(nc.vector.tensor_scalar(roots_plus[:], roots[:], 1.0, None, ALU.add))
            nc.vector.scalar_tensor_tensor(out=minus_means[:], in0=mean, scalar=-1.0, in1=roots[:],
                                           op0=ALU.mult, op1=ALU.mult).then_inc(roots_made, 1)

            with dve.Fori(0, WINDOWS // SEVEN) as i:
                for u in range(SEVEN):
                    w = i * SEVEN + u
                    nc.vector.tensor_scalar(state(2, w), state(3, w), moment[:, bass.ds(w * 2, 1)],
                                            roots[:, bass.ds(w, 1)], ALU.subtract, ALU.mult).then_inc(x1_ln_made, 1)
            def add_bias(w, v):
                dve.wait_ge(mlp2_summed, w + 1)
                dve.nop(nofuse=True)
                nc.vector.tensor_tensor(state(0, w), mlp2_ps[:, v % 2, 0:DIM], b2_all, ALU.add).then_inc(biased_made, 1)

            for i in range(WINDOWS // SEVEN):
                dve.wait_ge(products_made, i + 1)
                nc.vector.tensor_reduce(mlp_weight[:, i * SEVEN:(i + 1) * SEVEN], product(i), AX,
                                        ALU.add).then_inc(router_made, 1)
                v = i + BLOCK - WINDOWS // SEVEN
                if v >= 0:
                    add_bias(v, v)
            dve.wait_ge(router_made, SEVEN)

            link(nc.vector.tensor_scalar(mlp_weight[:], mlp_weight[:], br_all, None, ALU.add))
            link(nc.vector.tensor_copy(found[:], mlp_weight[:]))
            link(nc.vector.tensor_reduce(search[:, 0:1], below[:, 0:TAIL], AX, ALU.add))
            link(nc.vector.tensor_scalar(search[:, 1:2], search[:, 0:1], 0.5, None, ALU.is_gt))
            last_w = found[:, WINDOWS - 1:WINDOWS]
            link(nc.vector.tensor_tensor(search[:, 1:2], search[:, 1:2], ident[:, TAIL - 1:TAIL], ALU.add))
            link(nc.vector.tensor_tensor(last_w, last_w, search[:, 1:2], ALU.mult))
            link(nc.vector.tensor_scalar(search[:, 2:3], search[:, 1:2], 1.0, -LOWEST, ALU.subtract, ALU.mult))
            link(nc.vector.tensor_tensor(last_w, last_w, search[:, 2:3], ALU.add))

            magnitude = search[:, 3:4].bitcast(I32)
            candidate = search[:, 4:5].bitcast(I32)
            bit = search[:, 5:6].bitcast(I32)
            signed = search[:, 6:7]
            count = search[:, 7:8]
            enough = search[:, 8:9]
            sign = search[:, 9:10]
            flip = search[:, 10:11]
            keep = search[:, 11:12]
            asked = [0]

            def total(against, op, values=found):
                link(nc.vector.tensor_scalar(equals[:], values[:], against, None, op))
                nc.vector.tensor_reduce(count, equals[:], AX, ALU.add).then_inc(counts_made, 1)
                asked[0] += 1
                dve.wait_ge(totals_made, asked[0])

            link(nc.vector.memset(search[:, 12:13], 0.0))
            total(search[:, 12:13], ALU.is_ge)
            link(nc.vector.tensor_scalar(enough, total_ps, float(SELECTED), None, ALU.is_ge))
            link(nc.vector.tensor_scalar(sign, enough, 2.0, -1.0, ALU.mult, ALU.add))
            link(nc.vector.tensor_scalar(flip, enough, -1.0, 1.0, ALU.mult, ALU.add))
            link(nc.vector.memset(magnitude, 0))
            link(nc.vector.memset(bit, 1 << 30))

            asked_before = asked[0]

            def try_bit(i):
                link(nc.vector.tensor_tensor(candidate, magnitude, bit, ALU.bitwise_or))
                link(nc.vector.tensor_tensor(signed, search[:, 4:5], sign, ALU.mult))
                link(nc.vector.tensor_scalar(equals[:], found[:], signed, None, ALU.is_ge))
                nc.vector.tensor_reduce(count, equals[:], AX, ALU.add).then_inc(counts_made, 1)
                dve.wait_ge(totals_made, i + (asked_before + 1))
                link(nc.vector.tensor_scalar(enough, total_ps, float(SELECTED), None, ALU.is_ge))
                link(nc.vector.tensor_tensor(keep, enough, flip, ALU.not_equal))
                link(nc.vector.tensor_scalar(search[:, 13:14].bitcast(I32), keep, -1.0, None, ALU.mult))
                link(nc.vector.tensor_tensor(search[:, 14:15].bitcast(I32), bit, search[:, 13:14].bitcast(I32),
                                             ALU.bitwise_and))
                link(nc.vector.tensor_tensor(magnitude, magnitude, search[:, 14:15].bitcast(I32), ALU.bitwise_or))
                link(nc.vector.tensor_single_scalar(bit, bit, 1, op=ALU.logical_shift_right))

            def search_block(b):
                for i in range(TRIES):
                    try_bit(b * TRIES + i)
                for v in range(BLOCK):
                    add_bias((b + 1) * BLOCK + v, v)

            rolled_links(SEARCH_BLOCKS, search_block, 1)
            asked[0] += SEARCH_BLOCKS * TRIES
            link(nc.vector.tensor_tensor(signed, search[:, 3:4], sign, ALU.mult))
            link(nc.vector.tensor_scalar(equals[:], found[:], signed, None, ALU.is_ge))
            link(nc.vector.tensor_scalar(prefix[:], found[:], signed, None, ALU.is_gt))
            link(nc.vector.tensor_tensor(chosen[:], equals[:], prefix[:], ALU.subtract))
            link(nc.vector.scalar_tensor_tensor(out=prefix[:], in0=chosen[:], scalar=flip, in1=prefix[:],
                                                op0=ALU.mult, op1=ALU.add))
            link(nc.vector.tensor_copy(chosen[:], prefix[:]))
            link(nc.vector.tensor_copy(search[:, 12:13].bitcast(I32), flip))
            link(nc.vector.tensor_scalar(search[:, 13:14].bitcast(I32), magnitude, 65535, None, ALU.bitwise_and))
            link(nc.vector.tensor_scalar(search[:, 14:15].bitcast(I32), magnitude, 16, None, ALU.logical_shift_right))
            link(nc.vector.tensor_tensor(search[:, 13:14].bitcast(I32), search[:, 13:14].bitcast(I32),
                                         search[:, 12:13].bitcast(I32), ALU.add))
            link(nc.vector.tensor_scalar(search[:, 12:13].bitcast(I32), search[:, 13:14].bitcast(I32), 16, None,
                                         ALU.logical_shift_right))
            link(nc.vector.tensor_tensor(search[:, 14:15].bitcast(I32), search[:, 14:15].bitcast(I32),
                                         search[:, 12:13].bitcast(I32), ALU.add))
            link(nc.vector.tensor_scalar(search[:, 14:15].bitcast(I32), search[:, 14:15].bitcast(I32), 16, None,
                                         ALU.logical_shift_left))
            link(nc.vector.tensor_scalar(search[:, 13:14].bitcast(I32), search[:, 13:14].bitcast(I32), 65535, None,
                                         ALU.bitwise_and))
            link(nc.vector.tensor_tensor(search[:, 15:16].bitcast(I32), search[:, 14:15].bitcast(I32),
                                         search[:, 13:14].bitcast(I32), ALU.bitwise_or))
            link(nc.vector.tensor_tensor(signed, search[:, 15:16], sign, ALU.mult))
            link(nc.vector.tensor_scalar(equals[:], found[:], signed, None, ALU.is_equal))
            nc.vector.tensor_reduce(count, chosen[:], AX, ALU.add).then_inc(counts_made, 1)
            asked[0] += 1
            dve.wait_ge(totals_made, asked[0])
            link(nc.vector.tensor_scalar(keep, total_ps, -1.0, float(SELECTED), ALU.mult, ALU.add))
            nc.vector.engine_nop().then_inc(chosen_made, 1)
            dve.wait_ge(chosen_made, 2)
            link(nc.vector.tensor_copy(prefix[:], equals_ps[:, 0:WINDOWS]))
            link(nc.vector.memset(half_degree[:], 1.0))
            link(nc.vector.tensor_tensor_scan(out=half_degree[:], data0=half_degree[:],
                                              data1=prefix[:], initial=0.0, op0=ALU.mult, op1=ALU.add))
            link(nc.vector.tensor_tensor(half_degree[:], half_degree[:], prefix[:], ALU.subtract))
            link(nc.vector.tensor_tensor(prefix[:], half_degree[:], equals_ps[:, WINDOWS:2 * WINDOWS], ALU.add))
            link(nc.vector.tensor_scalar(prefix[:], prefix[:], keep, None, ALU.is_lt))
            link(nc.vector.tensor_tensor(prefix[:], prefix[:], equals[:], ALU.mult))
            link(nc.vector.tensor_tensor(chosen[:], chosen[:], prefix[:], ALU.add))
            link(nc.vector.tensor_tensor(chosen[:], chosen[:], mlp_weight[:], ALU.mult))

            def result(w):
                nc.vector.scalar_tensor_tensor(out=state(3, w), in0=state(0, w), scalar=chosen[:, bass.ds(w, 1)],
                                               in1=state(3, w), op0=ALU.mult, op1=ALU.add).then_inc(result_made, 1)

            searched = (SEARCH_BLOCKS + 1) * BLOCK
            dve.wait_ge(x1_plus_made, searched)
            dve.wait_ge(biased_made, searched)
            with dve.Fori(0, searched) as w:
                result(w)

            def finish_block(b, windows):
                for v in range(windows):
                    w = b * BLOCK + v
                    add_bias(w, v)
                    dve.wait_ge(biased_made, w + 1)
                    dve.wait_ge(x1_plus_made, w + 1)
                    dve.nop(nofuse=True)
                    result(w)

            with dve.Fori(SEARCH_BLOCKS + 1, BLOCKS) as b:
                finish_block(b, BLOCK)
            finish_block(BLOCKS, 1)

        @block.tensor
        def _(pe):
            pe.sem_inc(edge_multiplied, RING)
            pe.wait_ge(consts_made, CONSTS)
            pe.wait_ge(node_weights_landed, 16 * 3)

            def turn(w, u):
                pe.wait_ge(normal_made, w + 1)
                after(pe, normal_T_made, w - 1)
                for c in range(CH):
                    last = nc.tensor.transpose(turned_ps[u % 2][:, c * P:(c + 1) * P],
                                               normal[u][:, c * P:(c + 1) * P], ident[:])
                last.then_inc(normal_turned, 1)

            def project(w, u):
                pe.wait_ge(normal_T_made, w + 1)
                after(pe, h0_made, w - 1)
                for c in range(CH):
                    last = nc.tensor.matmul(h0_ps[u % 2], normal_T[u % 2][:, c * P:(c + 1) * P], wx_sb[:, c, :],
                                            start=(c == 0), stop=(c == CH - 1))
                last.then_inc(h0_summed, 1)

            def node_steps(first, n):
                for u in range(n):
                    turn(first + u, u)
                    if u:
                        project(first + u - 1, u - 1)
                project(first + n - 1, n - 1)

            in_two_parts(pe, node_steps)
            pe.wait_ge(h0_made, WINDOWS)

            for k in range(HOPS):
                width = WCOL if k == 0 else DIM

                def multiply_edges(it, u):
                    r = u % RING
                    use = it * (UNROLL // RING) + u // RING + k * (GROUPS // RING)
                    pe.wait_ge(edge_landed[r], (use + 1) * 16)
                    pe.wait_ge(added, it * UNROLL + (u + k * GROUPS + RING - 1))
                    for h in range(2):
                        part = slice(h * EDGE_DIM, (h + 1) * EDGE_DIM)
                        for j in range(2):
                            q = 2 * h + j
                            last = nc.tensor.matmul(e_ps[:, u % 2, q * DIM:(q + 1) * DIM], edge_ring[part, r, j, :],
                                                    we_sb[part, :], start=True, stop=True)
                    last.then_inc(edge_multiplied, 1)

                def scatter(it, u, w, slot):
                    if slot == EXTRA:
                        pe.wait_ge(extra_ready, w + k * (WINDOWS - 1))
                    else:
                        pe.wait_ge(onehot_ready, it * UNROLL + (u + k * GROUPS + 1))
                    for t in range(TILES_IN_GROUP):
                        last = nc.tensor.matmul(visit_ps[slot][:, 0:width], onehot[:, slot, t, :],
                                                messages[:, u % 2, t, 0:width], start=(t == 0),
                                                stop=(t == TILES_IN_GROUP - 1))
                    last.then_inc(scattered, 1)

                def walk(it, last):
                    ws = load_windows(pe, it)
                    for u in range(UNROLL):
                        if not last or u + 1 < UNROLL:
                            multiply_edges(it, u + 1)
                        pe.wait_ge(relued, it * UNROLL + (u + k * GROUPS + 3))
                        scatter(it, u, ws[u], u % 2)
                        with pe.If(ws[u] < ws[u + 1]):
                            scatter(it, u, next_window(ws[u]), EXTRA)
                            with pe.If(ws[u] + 1 < ws[u + 1]):
                                with pe.Fori(ws[u] + 2, ws[u + 1] + 1) as w:
                                    scatter(it, u, w, EXTRA)

                if k == 0:
                    pe.wait_ge(window_table_made, 1)
                multiply_edges(0, 0)
                with pe.Fori(0, GROUPS // UNROLL - 1) as it:
                    walk(it, False)
                walk(GROUPS // UNROLL - 1, True)

            def turn_attended(w, p):
                pe.wait_ge(attended_made, w + 1)
                for c in range(CH):
                    last = nc.tensor.transpose(attended_T_ps[:, c * P:(c + 1) * P], attended[p][:, c * P:(c + 1) * P],
                                               ident[:])
                last.then_inc(attended_turned, 1)

            def feed(w, p):
                pe.wait_ge(attended_T_made, w + 1)
                for j in range(FFJ):
                    for c in range(CH):
                        last = nc.tensor.matmul(hidden_ps[:, j * P:(j + 1) * P], wff1_sb[:, c, j * P:(j + 1) * P],
                                                attended_T[:, c * P:(c + 1) * P], start=(c == 0), stop=(c == CH - 1))
                last.then_inc(hidden_summed, 1)

            def feed_hidden(w, p):
                pe.wait_ge(hidden_made, w + 1)
                after(pe, x1_made, w)
                for j in range(FFJ):
                    last = nc.tensor.matmul(ffsum_ps, hidden_T[:, j * P:(j + 1) * P], wff2_sb[:, j, :],
                                            start=(j == 0), stop=(j == FFJ - 1))
                last.then_inc(ff_summed, 1)

            def attend_step(i, p):
                stage(turn_attended, i - 2, p)
                stage(feed_hidden, i - 3, 1 - p)
                stage(feed, i - 2, p)

            pe.wait_ge(window_done, WINDOWS * HOPS)
            pe.wait_ge(weights_landed, 16 * 5)
            in_pairs(pe, attend_step)

            def turn_x1(b, windows):
                after(pe, x1_T_made, b)
                pe.wait_ge(x1_staged, b + 1)
                for v in range(windows):
                    for c in range(CH):
                        last = nc.tensor.transpose(x1_T_ps[:, v * DIM + c * P:v * DIM + (c + 1) * P],
                                                   x1_block[:, v * DIM + c * P:v * DIM + (c + 1) * P], ident[:])
                last.then_inc(x1_turned, 1)

            def sum_counts():
                nc.tensor.matmul(total_ps, ones[:], search[:, 7:8], start=True, stop=True).then_inc(totals_made, 1)

            def mlp(b, windows, tries=0, more=0):
                n = windows * P
                pe.wait_ge(x1_T_made, b + 1)
                for j in range(HJ):
                    after(pe, gelu_made, b * HJ + j - 1)
                    for c in range(CH):
                        if windows == 1:
                            rhs = even_flat[:, b * BLOCK * DIM + c * P:b * BLOCK * DIM + (c + 1) * P]
                        else:
                            rhs = even_flat[:, bass.ds(b * (BLOCK * DIM), BLOCK * DIM)].rearrange(
                                "p (v d) -> p v d", v=BLOCK)[:, :, c * P:(c + 1) * P]
                        last = nc.tensor.matmul(mlp1_ps[:, j % 2, 0:n], w1_sb[:, c, j * P:(j + 1) * P], rhs,
                                                start=(c == 0), stop=(c == CH - 1))
                    last.then_inc(mlp1_summed, 1)
                    if tries and j % 2:
                        pe.wait_ge(counts_made, (b - 1) * tries + (j // 2 + 2))
                        sum_counts()
                if more:
                    turn_x1(b + 1, more)
                pe.wait_ge(gelu_made, b * HJ + HJ)
                for v in range(windows):
                    after(pe, biased_made, b * BLOCK + v - 1)
                    for j in range(HJ):
                        last = nc.tensor.matmul(mlp2_ps[:, v % 2, 0:DIM], hidden2_T[:, j, v * P:(v + 1) * P],
                                                w2_sb[:, j, :], start=(j == 0), stop=(j == HJ - 1))
                    last.then_inc(mlp2_summed, 1)

            turn_x1(0, BLOCK)
            mlp(0, BLOCK, more=BLOCK)
            pe.wait_ge(counts_made, 1)
            sum_counts()
            with pe.Fori(1, SEARCH_BLOCKS + 1) as b:
                mlp(b, BLOCK, TRIES, BLOCK)
            pe.wait_ge(counts_made, 2 + SEARCH_BLOCKS * TRIES)
            sum_counts()
            pe.wait_ge(chosen_made, 1)
            nc.tensor.matmul(equals_ps[:, 0:WINDOWS], ones[:], equals[:], start=True, stop=True)
            nc.tensor.matmul(equals_ps[:, WINDOWS:2 * WINDOWS], below[:], equals[:], start=True,
                             stop=True).then_inc(chosen_made, 1)
            with pe.Fori(SEARCH_BLOCKS + 1, BLOCKS - 1) as b:
                mlp(b, BLOCK, more=BLOCK)
            mlp(BLOCKS - 1, BLOCK, more=1)
            mlp(BLOCKS, 1)


def kernel(x, src, dst, edge_attr_64, L0_gnn_W_x, L0_gnn_W_e, L0_gnn_att_a, L0_gnn_W_ff1, L0_gnn_W_ff2,
           L0_ffn_attention_mask, L0_ffn_wr, L0_ffn_br, L0_ffn_w1, L0_ffn_b1, L0_ffn_w2, L0_ffn_b2):
    import numpy as np
    import concourse.bacc as bacc
    from concourse.bass_utils import run_bass_kernel_spmd

    def padded(a, fill):
        a = np.asarray(a)
        return np.concatenate([a, np.full((EP - E,) + a.shape[1:], fill, a.dtype)])

    src_p, dst_p = padded(src, 0), padded(dst, NP - 1)
    edges = padded(edge_attr_64, 0).reshape(GROUPS, 2, 2, P, EDGE_DIM).transpose(1, 4, 0, 2, 3)
    arrays = {
        "x": x, "src": src_p.reshape(TILES, P).T, "dst": dst_p.reshape(TILES, P).T,
        "group_last": dst_p[GROUP - 1::GROUP].reshape(1, GROUPS),
        "edges": edges.reshape(2 * EDGE_DIM, GROUPS * 2 * P),
        "W_x": L0_gnn_W_x, "W_e": L0_gnn_W_e, "att": np.asarray(L0_gnn_att_a).reshape(1, DIM),
        "W_ff1": L0_gnn_W_ff1, "W_ff2": L0_gnn_W_ff2, "wr": np.asarray(L0_ffn_wr).reshape(1, DIM),
        "br": np.asarray(L0_ffn_br).reshape(1, 1), "w1": L0_ffn_w1, "b1": L0_ffn_b1, "w2": L0_ffn_w2,
        "b2": np.asarray(L0_ffn_b2).reshape(1, DIM),
    }
    arrays = {name: np.ascontiguousarray(a) for name, a in arrays.items()}
    nc = bacc.Bacc("TRN2", target_bir_lowering=False, num_devices=1)
    args = [nc.dram_tensor(name, a.shape, mybir.dt.from_np(a.dtype), kind="ExternalInput").ap()
            for name, a in arrays.items()]
    out = nc.dram_tensor("out", (N, DIM), F32, kind="ExternalOutput").ap()
    build(nc, *args, out)
    return run_bass_kernel_spmd(nc, [arrays], core_ids=[0]).results[0]["out"]
```
